# Optimizing a Trainium2 kernel written in Bass

```python
import numpy as np
import jax
import jax.numpy as jnp

def _softmax(x, axis=-1):
    return jax.nn.softmax(x, axis=axis)

def _gelu(x):
    return jax.nn.gelu(x, approximate=True)

def _silu(x):
    return jax.nn.silu(x)

def _sigmoid(x):
    return jax.nn.sigmoid(x)

def _layernorm(x, axis=-1, eps=1e-05):
    m = jnp.mean(x, axis=axis, keepdims=True)
    v = jnp.var(x, axis=axis, keepdims=True)
    return (x - m) / jnp.sqrt(v + eps)

def _scatter_add(tgt, idx, src, axis=0):
    return tgt.at[idx].add(src)

def _segment_sum(src, seg, n):
    return jax.ops.segment_sum(src, seg, n)
kernel_name = 'mk_adj_resnorm_d1_adj_r2_7db58c'

def setup_inputs(seed: int=0):
    np.random.seed(seed)
    _w = jnp.asarray

    def _rec_inputs():
        import jax
        import jax.numpy as jnp
        _gk = jax.random.key(seed)
        x = -0.0004039 + 1 * jax.random.normal(jax.random.fold_in(_gk, 1), (64, 128, 384), jnp.float32)
        _w = (1.0 + jnp.arange(128, dtype=jnp.float32)) ** (-0.5)
        _w = _w / _w.mean()
        _pij = jnp.clip(0.015625 * _w[:, None] * _w[None, :], 0.0, 1.0)
        _a = jax.random.uniform(jax.random.fold_in(_gk, 2), (64, 128, 128)) < _pij
        _af = _a.astype(jnp.float32)
        adj = _af
        return (x, adj)
    x, adj = _rec_inputs()

    def _L0_gnn_setup():
        import jax, jax.numpy as jnp
        import numpy as np
        B, S, H, L = (32, 256, 384, 2)

        def _layer_norm(z, a, b, eps=0.001):
            mu = jnp.mean(z, axis=-1, keepdims=True)
            sigma = jnp.std(z, axis=-1, keepdims=True, ddof=1)
            return (z - mu) / (sigma + eps) * a + b
        key = jax.random.key(seed)
        ks = jax.random.split(key, 6)
        hidden_state = jax.random.normal(ks[0], (B, S, H), dtype=jnp.float32)
        adjacency_matrix = (jax.random.uniform(ks[1], (B, S, S)) < 0.2).astype(jnp.float32)
        W_left = 0.05 * jax.random.normal(ks[2], (L, H, H), dtype=jnp.float32)
        W_right = 0.05 * jax.random.normal(ks[3], (L, H, H), dtype=jnp.float32)
        W_lin = 0.05 * jax.random.normal(ks[4], (L, H, H), dtype=jnp.float32)
        b_lin = jnp.zeros((L, H), dtype=jnp.float32)
        ln_a = jnp.ones((L, H), dtype=jnp.float32)
        ln_b = jnp.zeros((L, H), dtype=jnp.float32)
        return {'hidden_state': hidden_state, 'adjacency_matrix': adjacency_matrix, 'W_left': W_left, 'W_right': W_right, 'W_lin': W_lin, 'b_lin': b_lin, 'ln_a': ln_a, 'ln_b': ln_b}
    _L0_gnn_all = _L0_gnn_setup()
    _L0_gnn_in = {k: v for k, v in _L0_gnn_all.items() if k in ('W_left', 'W_right', 'W_lin', 'b_lin', 'ln_a', 'ln_b')}
    del _L0_gnn_all
    return {'x': x, 'adj': adj, 'L0_gnn_W_left': _L0_gnn_in['W_left'], 'L0_gnn_W_right': _L0_gnn_in['W_right'], 'L0_gnn_W_lin': _L0_gnn_in['W_lin'], 'L0_gnn_b_lin': _L0_gnn_in['b_lin'], 'L0_gnn_ln_a': _L0_gnn_in['ln_a'], 'L0_gnn_ln_b': _L0_gnn_in['ln_b']}

def reference(x, adj, L0_gnn_W_left, L0_gnn_W_right, L0_gnn_W_lin, L0_gnn_b_lin, L0_gnn_ln_a, L0_gnn_ln_b):
    import jax
    import jax.numpy as jnp

    def _L0_gnn_ref(hidden_state, adjacency_matrix, W_left, W_right, W_lin, b_lin, ln_a, ln_b):
        import jax, jax.numpy as jnp
        import numpy as np
        B, S, H, L = (32, 256, 384, 2)

        def _layer_norm(z, a, b, eps=0.001):
            mu = jnp.mean(z, axis=-1, keepdims=True)
            sigma = jnp.std(z, axis=-1, keepdims=True, ddof=1)
            return (z - mu) / (sigma + eps) * a + b
        temper = float(np.sqrt(H))
        adj = adjacency_matrix
        adj_tri = jnp.triu(adj, k=1)
        diag_mask = jnp.triu(adj, k=0) - adj_tri
        h = hidden_state
        for l in range(L):
            m_left = jnp.einsum('bsh,oh->bso', h, W_left[l])
            m_right = jnp.einsum('bsh,oh->bso', h, W_right[l])
            u_left = jnp.einsum('bih,bjh->bij', h, m_left) / temper
            u_right = jnp.einsum('bih,bjh->bij', h, m_right) / temper
            u = u_left * adj_tri + u_left * diag_mask + u_right * jnp.swapaxes(adj_tri, 1, 2)
            delta_exp_u = jnp.exp(u) * adj
            attention = delta_exp_u / (jnp.sum(delta_exp_u, axis=2, keepdims=True) + 1e-10)
            h_lin = jnp.einsum('bsh,oh->bso', h, W_lin[l]) + b_lin[l]
            ctx = jnp.matmul(attention, h_lin)
            h = jax.nn.relu(_layer_norm(ctx, ln_a[l], ln_b[l]))
        return h
    x = _layernorm(x + _L0_gnn_ref(x, adj, L0_gnn_W_left, L0_gnn_W_right, L0_gnn_W_lin, L0_gnn_b_lin, L0_gnn_ln_a, L0_gnn_ln_b), axis=-1)
    return x

_drawn_inputs = setup_inputs


def setup_inputs(seed=0):
    import zlib

    import numpy as np

    out = dict(_drawn_inputs(seed))
    spreads = {'L0_gnn_b_lin': (0.0, 0.1), 'L0_gnn_ln_a': (1.0, 0.2), 'L0_gnn_ln_b': (0.0, 0.1)}
    factors = {}
    for name, (base, spread) in spreads.items():
        noise = np.random.default_rng([zlib.crc32(name.encode()), seed]).standard_normal(out[name].shape)
        drawn = base * np.exp(spread * noise) if base else spread * noise
        out[name] = jnp.asarray(drawn.astype(out[name].dtype))
    for name, factor in factors.items():
        out[name] = (out[name] * factor).astype(out[name].dtype)
    return out
```

```python
from contextlib import ExitStack

import concourse.bass as bass
from concourse import mybir

F32 = mybir.dt.float32
F32R = mybir.dt.float32r
ALU = mybir.AluOpType
ACT = mybir.ActivationFunctionType
AX = mybir.AxisListType

B, S, H, L = 64, 128, 384, 2
P = 128
G = 512 // S
NG = B // G
HC = H // P
TOK = G * S
TEMPER = float(H) ** 0.5
LN_EPS = 1e-3
SUM_EPS = 1e-10
OUT_EPS = 1e-5
M_TILES = 2 * HC
UNIT_TILES = M_TILES + G
LEFT, RIGHT, LIN = range(3)
DMA = 16


class Slot:

    def __init__(self, n, tile0, layer=None, prev_layer=None, prev_mask=None, transposes=None,
                 mask_group=None, mask_buf=None, split_group=None, final=None, final_buf=None,
                 prev_second=None, parity=0):
        self.n = n
        self.at = n if isinstance(n, int) else None
        self.tile0 = tile0
        self.layer = layer
        self.prev_layer = prev_layer
        self.prev_mask = prev_mask
        self.prev_second = prev_second
        self.transposes = transposes
        self.mask_group = mask_group
        self.mask_buf = mask_buf
        self.split_group = split_group
        self.final = final
        self.final_buf = final_buf
        self.parity = parity


PAIR_TILES = 2 * UNIT_TILES + HC


def odd_slot(k, k_parity, first=False):
    return Slot(2 * k + 1, PAIR_TILES * k + UNIT_TILES, layer=0,
                prev_layer=0 if first else 1, prev_mask=0 if first else 1 - k_parity,
                prev_second=None if first else k - 1, transposes=k,
                mask_group=k + 1, mask_buf=1 - k_parity, parity=1)


def even_slot(k, k_parity, first=False, last=False):
    return Slot(2 * k + 2, PAIR_TILES * k + 2 * UNIT_TILES + HC, layer=1,
                prev_layer=0, prev_mask=1 - k_parity,
                transposes=k + 1 if last else None,
                split_group=None if last else k + 2,
                final=None if first else k - 1, final_buf=None if first else 1 - k_parity,
                parity=0)


PAIRS = NG - 1
LOOPS = (PAIRS - 3) // 2
assert PAIRS == 3 + 2 * LOOPS


def head_slots():
    return [Slot(0, 0, layer=0, split_group=1, parity=0),
            odd_slot(0, 0, first=True), even_slot(0, 0, first=True),
            odd_slot(1, 1), even_slot(1, 1)]


def loop_slots(r):
    return [odd_slot(2 * r + 2, 0), even_slot(2 * r + 2, 0),
            odd_slot(2 * r + 3, 1), even_slot(2 * r + 3, 1)]


def tail_slots():
    k = PAIRS - 1
    n = 2 * PAIRS + 1
    return [odd_slot(k, k % 2), even_slot(k, k % 2, last=True),
            Slot(n, PAIR_TILES * PAIRS + UNIT_TILES + HC, layer=1, prev_layer=1,
                 prev_mask=(NG - 2) % 2, prev_second=NG - 2, parity=n % 2),
            Slot(n + 1, None, prev_layer=1, prev_mask=(NG - 1) % 2, prev_second=NG - 1,
                 final=NG - 2, final_buf=(NG - 2) % 2, parity=(n + 1) % 2),
            Slot(n + 2, None, final=NG - 1, final_buf=(NG - 1) % 2, parity=(n + 2) % 2)]


def drained_before(slot, t):
    return slot.tile0 + (t - 2 if t >= 3 else (0, -2, -1)[t])


def build(nc, x_tok, x_feat, adj_pair, w_feat, b_lin, ln_a, ln_b, identity_in, triangles_in, out):
    ctx = ExitStack()
    with ctx:
        def sb(name, shape, dt=F32):
            return ctx.enter_context(nc.sbuf_tensor(name, shape, dt))

        def psum(name, shape):
            return ctx.enter_context(nc.psum_tensor(name, shape, F32))

        def sem(name):
            return ctx.enter_context(nc.semaphore(name))

        identity = sb("identity", [P, S])
        triangles = sb("triangles", [P, 2, S])
        bias = sb("bias", [P, L, H])
        gain = sb("gain", [P, L, H])
        offset = sb("offset", [P, L, H])
        half = sb("half", [P, G])
        minus_half = sb("minus_half", [P, G])
        unbiased = sb("unbiased", [P, G])
        out_eps = sb("out_eps", [P, G])
        w_hi = sb("w_hi", [P, L, 3, HC, H], F32R)
        w_lo = sb("w_lo", [P, L, 3, HC, H], F32R)
        x_in = sb("x_in", [P, HC, TOK])
        adj = [sb(f"adj{i}", [P, 2, G, S]) for i in range(2)]
        gate = [sb(f"gate{i}", [P, 2, G, S]) for i in range(2)]
        residual = [sb(f"residual{i}", [P, G, H]) for i in range(2)]
        ht_hi = [sb(f"ht_hi{i}", [P, HC, TOK], F32R) for i in range(2)]
        ht_lo = [sb(f"ht_lo{i}", [P, HC, TOK], F32R) for i in range(2)]
        m_hi = sb("m_hi", [P, HC, 2, TOK], F32R)
        m_lo = sb("m_lo", [P, HC, 2, TOK], F32R)
        hlin = sb("hlin", [P, 2, H])
        hlin_hi = sb("hlin_hi", [P, G, H], F32R)
        hlin_lo = sb("hlin_lo", [P, G, H], F32R)
        gated = sb("gated", [P, 2, G, S])
        score = sb("score", [P, G, S])
        expd = sb("expd", [P, G, S])
        delta = sb("delta", [P, G, S])
        att_hi = sb("att_hi", [P, TOK], F32R)
        att_lo = sb("att_lo", [P, TOK], F32R)
        row_sum = sb("row_sum", [P, G])
        row_den = sb("row_den", [P, G])
        row_scale = sb("row_scale", [P, G])
        z = sb("z", [P, G, H])
        stats = sb("stats", [P, G, 6])
        moments = sb("moments", [P, G, 2])
        variance = sb("variance", [P, G])
        sigma = sb("sigma", [P, G])
        ln_den = sb("ln_den", [P, G])
        ln_scale = sb("ln_scale", [P, G])
        ln_shift = sb("ln_shift", [P, G])
        h1 = sb("h1", [P, G, H])
        h2 = sb("h2", [P, G, H])
        out_stats = sb("out_stats", [P, G, 6])
        out_moments = sb("out_moments", [P, G, 2])
        out_var = sb("out_var", [P, G])
        out_scale = sb("out_scale", [P, G])
        result = sb("result", [P, G, H])
        raw_w = [[b[:].rearrange("p b h -> p (b h)")[:, 0:HC * H].rearrange("p (c o) -> p c o", c=HC)
                  for b in bufs] for bufs in ((z, h1, h2), (residual[0], residual[1], result))]

        tile = [psum(f"tile{i}", [P, TOK]) for i in range(3)]
        u_bank = [psum(f"u_bank{i}", [P, 2, 2, S]) for i in range(2)]
        att_bank = psum("att_bank", [P, TOK])
        c_bank = [psum(f"c_bank{i}", [P, H]) for i in range(2)]

        w_in = [[sem(f"w_in{l}{k}") for k in range(3)] for l in range(L)]
        consts_in = sem("consts_in")
        x_landed = sem("x_landed")
        adj_landed = sem("adj_landed")
        residual_landed = [sem(f"residual_landed{i}") for i in range(2)]
        stored = sem("stored")
        tile_full = sem("tile_full")
        u_full = sem("u_full")
        att_full = sem("att_full")
        c_full = sem("c_full")
        w_hi_done = sem("w_hi_done")
        m_hi_done = sem("m_hi_done")
        hlin_hi_done = sem("hlin_hi_done")
        ht_hi_done = sem("ht_hi_done")
        exp_done = sem("exp_done")
        att_hi_done = sem("att_hi_done")
        z_done = sem("z_done")
        norm_done = sem("norm_done")
        tile_drained = sem("tile_drained")
        w_lo0_done = sem("w_lo0_done")
        x_hi_done = sem("x_hi_done")
        gated_done = sem("gated_done")
        score_done = sem("score_done")
        delta_done = sem("delta_done")
        row_sum_done = sem("row_sum_done")
        row_den_done = sem("row_den_done")
        row_scale_done = sem("row_scale_done")
        att_lo_done = sem("att_lo_done")
        stats_done = sem("stats_done")
        moments_done = sem("moments_done")
        ln_den_done = sem("ln_den_done")
        ln_scale_done = sem("ln_scale_done")
        ln_shift_done = sem("ln_shift_done")
        summed_done = sem("summed_done")
        out_stats_done = sem("out_stats_done")
        out_moments_done = sem("out_moments_done")
        result_done = sem("result_done")
        scalars_set = sem("scalars_set")
        w_lo1_done = sem("w_lo1_done")
        x_lo_done = sem("x_lo_done")
        gate_done = sem("gate_done")
        hlin_lo_done = sem("hlin_lo_done")
        variance_done = sem("variance_done")
        sigma_done = sem("sigma_done")
        gained_done = sem("gained_done")
        h_done = sem("h_done")
        out_var_done = sem("out_var_done")
        out_scale_done = sem("out_scale_done")

        block = ctx.enter_context(nc.Block())

        def chunk(b):
            return slice(b * S, (b + 1) * S)

        @block.sync
        def _(sp):
            sp.dma_start(raw_w[0][LEFT], w_feat[0, LEFT]).then_inc(w_in[0][LEFT], DMA)
            sp.dma_start(x_in[:], x_feat[0]).then_inc(x_landed, DMA)
            sp.dma_start(raw_w[0][RIGHT], w_feat[0, RIGHT]).then_inc(w_in[0][RIGHT], DMA)
            sp.dma_start(raw_w[0][LIN], w_feat[0, LIN]).then_inc(w_in[0][LIN], DMA)
            sp.dma_start(identity[:], identity_in).then_inc(consts_in, DMA)
            sp.dma_start(triangles[:], triangles_in).then_inc(consts_in, DMA)
            sp.dma_start(bias[:], b_lin.partition_broadcast(P)).then_inc(consts_in, DMA)
            sp.dma_start(gain[:], ln_a.partition_broadcast(P)).then_inc(consts_in, DMA)
            sp.dma_start(offset[:], ln_b.partition_broadcast(P)).then_inc(consts_in, DMA)
            sp.dma_start(adj[0][:], adj_pair[0]).then_inc(adj_landed, DMA)
            for kind in range(3):
                sp.dma_start(raw_w[1][kind], w_feat[1, kind]).then_inc(w_in[1][kind], DMA)
            sp.wait_ge(x_lo_done, 1)
            sp.dma_start(x_in[:], x_feat[1]).then_inc(x_landed, DMA)
            sp.wait_ge(adj_landed, DMA)
            sp.dma_start(adj[1][:], adj_pair[1]).then_inc(adj_landed, DMA)

            def load_x(k):
                sp.wait_ge(x_lo_done, k + 2)
                sp.dma_start(x_in[:], x_feat[k + 2]).then_inc(x_landed, DMA)

            def load_adj(k, k_parity):
                sp.wait_ge(delta_done, 2 * k + 1)
                sp.dma_start(adj[1 - k_parity][:], adj_pair[k + 1]).then_inc(adj_landed, DMA)

            def load_residual(k, k_parity):
                sp.dma_start(residual[k_parity][:], x_tok[k]).then_inc(residual_landed[k_parity], DMA)

            def store(g):
                sp.wait_ge(result_done, g + 1)
                sp.dma_start(out[g], result[:]).then_inc(stored, DMA)

            load_x(0)
            sp.wait_ge(w_lo1_done, 3)
            load_residual(0, 0)

            def pair(k, k_parity):
                load_x(k)
                load_adj(k, k_parity)
                load_residual(k, k_parity)
                store(k - 1)

            pair(1, 1)
            with sp.Fori(0, LOOPS) as r:
                pair(2 * r + 2, 0)
                pair(2 * r + 3, 1)
            k = PAIRS - 1
            load_adj(k, k % 2)
            load_residual(k, k % 2)
            store(k - 1)
            load_residual(NG - 1, (NG - 1) % 2)
            store(NG - 2)
            store(NG - 1)
            sp.wait_ge(stored, DMA * NG)

        @block.tensor
        def _(pe):
            def passes(dst, lhs_hi, lhs_lo, rhs_hi, rhs_lo, first, last):
                nc.tensor.matmul(dst, lhs_hi, rhs_hi, start=first, stop=False)
                nc.tensor.matmul(dst, lhs_hi, rhs_lo, start=False, stop=False)
                return nc.tensor.matmul(dst, lhs_lo, rhs_hi, start=False, stop=last)

            def project_tile(s, t):
                side, oc = t // HC, t % HC
                hi, lo = ht_hi[s.parity], ht_lo[s.parity]
                for hc in range(HC):
                    last = passes(tile[t % 3][:],
                                  w_hi[:, s.layer, side, hc, chunk(oc)],
                                  w_lo[:, s.layer, side, hc, chunk(oc)],
                                  hi[:, hc, :], lo[:, hc, :], hc == 0, hc == HC - 1)
                return last

            def slot(s):
                if s.layer is not None:
                    if s.at == 0:
                        pe.wait_ge(x_lo_done, 1)
                        for t in range(M_TILES):
                            if t % HC == 0:
                                pe.wait_ge(w_lo0_done, t // HC + 1)
                            if t >= 3:
                                pe.wait_ge(tile_drained, drained_before(s, t))
                            project_tile(s, t).then_inc(tile_full, 1)
                        pe.wait_ge(w_lo0_done, 3)
                    else:
                        if s.layer == 0:
                            pe.wait_ge(x_lo_done, s.mask_group + 1)
                        elif s.at == 2:
                            pe.wait_ge(w_lo1_done, 3)
                        for t in range(HC):
                            pe.wait_ge(tile_drained, drained_before(s, t))
                            project_tile(s, t).then_inc(tile_full, 1)
                if s.prev_layer is not None:
                    pe.wait_ge(delta_done, s.n)
                    if s.at == 1:
                        pe.wait_ge(consts_in, 5 * DMA)
                    else:
                        pe.wait_ge(att_lo_done, s.n - 1)
                    for b in range(G):
                        last = nc.tensor.transpose(att_bank[:, chunk(b)], delta[:, b, :], identity[:])
                    last.then_inc(att_full, 1)
                if s.layer is not None and s.at != 0:
                    for t in range(HC, M_TILES):
                        pe.wait_ge(tile_drained, drained_before(s, t))
                        project_tile(s, t).then_inc(tile_full, 1)
                hi, lo = ht_hi[s.parity], ht_lo[s.parity]

                def context(b):
                    if s.at != 1 or b >= 2:
                        pe.wait_ge(z_done, G * (s.n - 1) + b - 1)
                    passes(c_bank[b % 2][:], att_hi[:, chunk(b)], att_lo[:, chunk(b)],
                           hlin_hi[:, b, :], hlin_lo[:, b, :], True, True).then_inc(c_full, 1)

                def linear(b):
                    t = M_TILES + b
                    pe.wait_ge(tile_drained, drained_before(s, t))
                    for hc in range(HC):
                        last = passes(tile[t % 3][:, 0:H], hi[:, hc, chunk(b)], lo[:, hc, chunk(b)],
                                      w_hi[:, s.layer, LIN, hc, :], w_lo[:, s.layer, LIN, hc, :],
                                      hc == 0, hc == HC - 1)
                    last.then_inc(tile_full, 1)

                def transpose_h(hc):
                    t = UNIT_TILES + hc
                    pe.wait_ge(tile_drained, drained_before(s, t))
                    for b in range(G):
                        last = nc.tensor.transpose(tile[t % 3][:, chunk(b)], h1[:, b, chunk(hc)],
                                                   identity[:])
                    last.then_inc(tile_full, 1)

                def scores(b):
                    if b % 2 == 0 and s.at != 0:
                        pe.wait_ge(gated_done, 2 * (s.n - 1) + b // 2 + 1)
                    for hc in range(HC):
                        last = passes(u_bank[b // 2][:, b % 2, :, :], hi[:, hc, chunk(b)], lo[:, hc, chunk(b)],
                                      m_hi[:, hc, :, chunk(b)], m_lo[:, hc, :, chunk(b)],
                                      hc == 0, hc == HC - 1)
                    if b % 2 == 1:
                        last.then_inc(u_full, 1)

                if s.prev_layer is not None:
                    pe.wait_ge(att_lo_done, s.n)
                    pe.wait_ge(hlin_lo_done, G * s.n)
                    context(0)
                    context(1)
                if s.layer is not None:
                    linear(0)
                if s.prev_layer is not None:
                    context(2)
                    context(3)
                if s.layer is None:
                    return
                for b in range(1, G):
                    linear(b)
                if s.transposes is not None:
                    pe.wait_ge(h_done, s.n if s.at in (1, 2 * PAIRS) else s.n - 1)
                    transpose_h(0)
                    transpose_h(1)
                pe.wait_ge(tile_drained, s.tile0 + M_TILES)
                scores(0)
                if s.transposes is not None:
                    transpose_h(2)
                for b in range(1, G):
                    scores(b)

            for s in head_slots():
                slot(s)
            with pe.Fori(0, LOOPS) as r:
                for s in loop_slots(r):
                    slot(s)
            for s in tail_slots():
                slot(s)

        @block.scalar
        def _(act):
            def split_weights(layer):
                for kind in range(3):
                    act.wait_ge(w_in[layer][kind], DMA)
                    nc.scalar.activation(w_hi[:, layer, kind], raw_w[layer][kind], ACT.Copy)\
                      .then_inc(w_hi_done, 1)

            def slot(s):
                if s.prev_layer is not None:
                    act.wait_ge(score_done, s.n)
                    nc.scalar.activation(expd[:], score[:], ACT.Exp, scale=1.0 / TEMPER)\
                      .then_inc(exp_done, 1)
                if s.layer is not None:
                    for t in range(HC):
                        act.wait_ge(tile_full, s.tile0 + t + 1)
                        nc.scalar.activation(m_hi[:, t % HC, t // HC, :], tile[t % 3][:], ACT.Copy)\
                          .then_inc(m_hi_done, 1)
                if s.prev_layer is not None:
                    act.wait_ge(att_full, s.n)
                    nc.scalar.activation(att_hi[:], att_bank[:], ACT.Copy).then_inc(att_hi_done, 1)
                if s.layer is not None:
                    for t in range(HC, M_TILES):
                        act.wait_ge(tile_full, s.tile0 + t + 1)
                        nc.scalar.activation(m_hi[:, t % HC, t // HC, :], tile[t % 3][:], ACT.Copy)\
                          .then_inc(m_hi_done, 1)
                if s.prev_layer is not None:
                    act.wait_ge(row_scale_done, s.n)
                    if s.at != 1:
                        act.wait_ge(h_done, s.n - 1)
                    for b in range(G):
                        act.wait_ge(c_full, G * (s.n - 1) + b + 1)
                        nc.scalar.activation(z[:, b, :], c_bank[b % 2][:], ACT.Copy,
                                             scale=row_scale[:, b:b + 1]).then_inc(z_done, 1)

                def hlin_high(b):
                    act.wait_ge(tile_drained, s.tile0 + M_TILES + b + 1)
                    nc.scalar.activation(hlin_hi[:, b, :], hlin[:, b % 2, :], ACT.Copy)\
                      .then_inc(hlin_hi_done, 1)

                if s.layer is not None:
                    hlin_high(0)
                    hlin_high(1)
                if s.prev_layer is not None:
                    act.wait_ge(ln_shift_done, s.n)
                    for b in range(G):
                        last = nc.scalar.activation(z[:, b, :], z[:, b, :], ACT.Identity,
                                                    bias=ln_shift[:, b:b + 1], scale=ln_scale[:, b:b + 1])
                    last.then_inc(norm_done, 1)
                if s.layer is not None:
                    hlin_high(2)
                    hlin_high(3)
                if s.transposes is not None:
                    for hc in range(HC):
                        act.wait_ge(tile_full, s.tile0 + UNIT_TILES + hc + 1)
                        nc.scalar.activation(ht_hi[1 - s.parity][:, hc, :], tile[(UNIT_TILES + hc) % 3][:],
                                             ACT.Relu).then_inc(ht_hi_done, 1)

            split_weights(0)
            head = head_slots()
            slot(head[0])
            split_weights(1)
            for s in head[1:]:
                slot(s)
            with act.Fori(0, LOOPS) as r:
                for s in loop_slots(r):
                    slot(s)
            for s in tail_slots():
                slot(s)

        @block.vector
        def _(dve):
            def split_x(s, group, buf):
                dve.wait_ge(x_landed, DMA * (group + 1))
                nc.vector.tensor_copy(ht_hi[buf][:], x_in[:]).then_inc(x_hi_done, 1)

            def m_low(s, t):
                dve.wait_ge(m_hi_done, M_TILES * s.n + t + 1)
                nc.vector.tensor_tensor(m_lo[:, t % HC, t // HC, :], tile[t % 3][:],
                                        m_hi[:, t % HC, t // HC, :].bitcast(F32), ALU.subtract)\
                  .then_inc(tile_drained, 1)

            def slot(s):
                prev, unit, final = s.prev_layer is not None, s.layer is not None, s.final is not None
                if prev:
                    for k in range(2):
                        dve.wait_ge(u_full, 2 * (s.n - 1) + k + 1)
                        nc.vector.tensor_tensor(
                            gated[:, :, 2 * k:2 * k + 2, :],
                            u_bank[k][:].rearrange("p b s j -> p s b j"),
                            gate[s.prev_mask][:, :, 2 * k:2 * k + 2, :], ALU.mult).then_inc(gated_done, 1)
                    dve.wait_ge(gated_done, 2 * s.n)
                    nc.vector.tensor_tensor(score[:], gated[:, 0], gated[:, 1], ALU.add)\
                      .then_inc(score_done, 1)
                    dve.wait_ge(exp_done, s.n)
                    nc.vector.tensor_tensor(delta[:], expd[:], adj[s.prev_mask][:, 0], ALU.mult)\
                      .then_inc(delta_done, 1)
                if unit:
                    m_low(s, 0)
                if s.split_group is not None:
                    split_x(s, s.split_group, 1 - s.parity)
                if unit:
                    m_low(s, 1)
                if prev:
                    dve.wait_ge(delta_done, s.n)
                    nc.vector.reduce_sum(row_sum[:], delta[:], AX.X).then_inc(row_sum_done, 1)
                    dve.wait_ge(row_sum_done, s.n)
                    nc.vector.tensor_scalar(row_den[:], row_sum[:], SUM_EPS, None, ALU.add)\
                      .then_inc(row_den_done, 1)
                    dve.wait_ge(row_den_done, s.n)
                    nc.vector.reciprocal(row_scale[:], row_den[:]).then_inc(row_scale_done, 1)
                if final:
                    dve.wait_ge(residual_landed[s.final_buf], DMA // 2 * (s.final - s.final_buf) + DMA)
                    dve.wait_ge(h_done, s.n - 1)
                    res = residual[s.final_buf]
                    nc.vector.scalar_tensor_tensor(out=res[:], in0=h2[:], scalar=0.0, in1=res[:],
                                                   op0=ALU.max, op1=ALU.add).then_inc(summed_done, 1)
                if unit:
                    m_low(s, 2)
                if prev:
                    dve.wait_ge(att_hi_done, s.n)
                    nc.vector.tensor_tensor(att_lo[:], att_bank[:], att_hi[:].bitcast(F32), ALU.subtract)\
                      .then_inc(att_lo_done, 1)
                if final:
                    dve.wait_ge(summed_done, s.final + 1)
                    for b in range(G):
                        last = nc.vector.bn_stats(out_stats[:, b, :], res[:, b, :])
                    last.then_inc(out_stats_done, 1)
                    dve.wait_ge(out_stats_done, s.final + 1)
                if unit:
                    m_low(s, 3)
                if final:
                    for b in range(G):
                        last = nc.vector.bn_aggr(out_moments[:, b, :], out_stats[:, b, :])
                    last.then_inc(out_moments_done, 1)
                if unit:
                    m_low(s, 4)
                    m_low(s, 5)
                if final:
                    dve.wait_ge(out_scale_done, s.final + 1)
                    if s.at != 4:
                        dve.wait_ge(stored, DMA * s.final)
                    for b in range(G):
                        last = nc.vector.tensor_scalar(result[:, b, :], res[:, b, :],
                                                       out_moments[:, b, 0:1], out_scale[:, b:b + 1],
                                                       ALU.subtract, ALU.mult)
                    last.then_inc(result_done, 1)
                if prev:
                    for b in range(G):
                        dve.wait_ge(z_done, G * (s.n - 1) + b + 1)
                        nc.vector.bn_stats(stats[:, b, :], z[:, b, :]).then_inc(stats_done, 1)
                    dve.wait_ge(stats_done, G * s.n)

                def hlin_bias(b):
                    dve.wait_ge(tile_full, s.tile0 + M_TILES + b + 1)
                    if s.at != 0 or b >= 2:
                        dve.wait_ge(hlin_lo_done, G * s.n + b - 1)
                    nc.vector.tensor_tensor(hlin[:, b % 2, :], tile[(M_TILES + b) % 3][:, 0:H],
                                            bias[:, s.layer, :], ALU.add).then_inc(tile_drained, 1)

                if unit:
                    if s.at == 0:
                        dve.wait_ge(consts_in, 5 * DMA)
                    hlin_bias(0)
                if prev:
                    for b in range(G):
                        last = nc.vector.bn_aggr(moments[:, b, :], stats[:, b, :])
                    last.then_inc(moments_done, 1)
                if unit:
                    hlin_bias(1)
                if prev:
                    dve.wait_ge(sigma_done, s.n)
                    nc.vector.tensor_scalar(ln_den[:], sigma[:], LN_EPS, None, ALU.add)\
                      .then_inc(ln_den_done, 1)
                    dve.wait_ge(ln_den_done, s.n)
                    nc.vector.reciprocal(ln_scale[:], ln_den[:]).then_inc(ln_scale_done, 1)
                    dve.wait_ge(ln_scale_done, s.n)
                    nc.vector.scalar_tensor_tensor(out=ln_shift[:], in0=moments[:, :, 0], scalar=-1.0,
                                                   in1=ln_scale[:], op0=ALU.mult, op1=ALU.mult)\
                      .then_inc(ln_shift_done, 1)
                if unit:
                    hlin_bias(2)
                    hlin_bias(3)
                if s.transposes is not None:
                    for hc in range(HC):
                        dve.wait_ge(ht_hi_done, HC * s.transposes + hc + 1)
                        nc.vector.scalar_tensor_tensor(
                            out=ht_lo[1 - s.parity][:, hc, :], in0=tile[(UNIT_TILES + hc) % 3][:], scalar=0.0,
                            in1=ht_hi[1 - s.parity][:, hc, :].bitcast(F32), op0=ALU.max, op1=ALU.subtract)\
                          .then_inc(tile_drained, 1)

            split_x(None, 0, 0)
            for kind in range(3):
                dve.wait_ge(w_hi_done, kind + 1)
                nc.vector.tensor_tensor(w_lo[:, 0, kind], raw_w[0][kind], w_hi[:, 0, kind].bitcast(F32),
                                        ALU.subtract).then_inc(w_lo0_done, 1)
            for s in head_slots():
                slot(s)
            with dve.Fori(0, LOOPS) as r:
                for s in loop_slots(r):
                    slot(s)
            for s in tail_slots():
                slot(s)

        @block.gpsimd
        def _(pool):
            def split_x(group, buf):
                pool.wait_ge(x_hi_done, group + 1)
                nc.gpsimd.tensor_tensor(ht_lo[buf][:], x_in[:], ht_hi[buf][:].bitcast(F32),
                                        ALU.subtract).then_inc(x_lo_done, 1)

            def mask(group, buf):
                pool.wait_ge(adj_landed, DMA * (group + 1))
                nc.gpsimd.tensor_tensor(gate[buf][:], adj[buf][:],
                                        triangles[:].unsqueeze(2).to_broadcast([P, 2, G, S]),
                                        ALU.mult).then_inc(gate_done, 1)

            def slot(s):
                prev, unit, final = s.prev_layer is not None, s.layer is not None, s.final is not None
                if s.split_group is not None:
                    split_x(s.split_group, 1 - s.parity)
                if s.mask_group is not None:
                    mask(s.mask_group, s.mask_buf)
                if final:
                    pool.wait_ge(out_moments_done, s.final + 1)
                    nc.gpsimd.tensor_tensor(out_var[:], out_moments[:, :, 1], out_eps[:], ALU.add)\
                      .then_inc(out_var_done, 1)
                    pool.wait_ge(out_var_done, s.final + 1)
                    nc.gpsimd.tensor_tensor(out_scale[:], out_var[:], minus_half[:], ALU.pow)\
                      .then_inc(out_scale_done, 1)
                if prev:
                    pool.wait_ge(moments_done, s.n)
                    nc.gpsimd.tensor_tensor(variance[:], moments[:, :, 1], unbiased[:], ALU.mult)\
                      .then_inc(variance_done, 1)
                    pool.wait_ge(variance_done, s.n)
                    nc.gpsimd.tensor_tensor(sigma[:], variance[:], half[:], ALU.pow)\
                      .then_inc(sigma_done, 1)

                def hlin_low(b):
                    pool.wait_ge(hlin_hi_done, G * s.n + b + 1)
                    nc.gpsimd.tensor_tensor(hlin_lo[:, b, :], hlin[:, b % 2, :],
                                            hlin_hi[:, b, :].bitcast(F32), ALU.subtract)\
                      .then_inc(hlin_lo_done, 1)

                if unit:
                    hlin_low(0)
                    hlin_low(1)
                if prev:
                    pool.wait_ge(norm_done, s.n)
                    wide = [P, G, H]
                    a = gain[:, s.prev_layer:s.prev_layer + 1, :].to_broadcast(wide)
                    nc.gpsimd.tensor_tensor(z[:], z[:], a, ALU.mult).then_inc(gained_done, 1)
                if unit:
                    hlin_low(2)
                    hlin_low(3)
                if prev:
                    pool.wait_ge(gained_done, s.n)
                    b_ = offset[:, s.prev_layer:s.prev_layer + 1, :].to_broadcast(wide)
                    if s.prev_layer == 1:
                        pool.wait_ge(summed_done, s.prev_second)
                    dst = h2 if s.prev_layer else h1
                    nc.gpsimd.tensor_tensor(dst[:], z[:], b_, ALU.add).then_inc(h_done, 1)

            for constant, value in ((half, 0.5), (minus_half, -0.5), (unbiased, H / (H - 1.0)),
                                    (out_eps, OUT_EPS)):
                nc.gpsimd.memset(constant[:], value).then_inc(scalars_set, 1)
            split_x(0, 0)
            pool.wait_ge(consts_in, 5 * DMA)
            mask(0, 0)
            pool.wait_ge(scalars_set, 4)
            head = head_slots()
            slot(head[0])
            for kind in range(3):
                pool.wait_ge(w_hi_done, 3 + kind + 1)
                nc.gpsimd.tensor_tensor(w_lo[:, 1, kind], raw_w[1][kind], w_hi[:, 1, kind].bitcast(F32),
                                        ALU.subtract).then_inc(w_lo1_done, 1)
            for s in head[1:]:
                slot(s)
            with pool.Fori(0, LOOPS) as r:
                for s in loop_slots(r):
                    slot(s)
            for s in tail_slots():
                slot(s)


def kernel(x, adj, L0_gnn_W_left, L0_gnn_W_right, L0_gnn_W_lin, L0_gnn_b_lin, L0_gnn_ln_a, L0_gnn_ln_b):
    import numpy as np
    import concourse.bacc as bacc
    from concourse.bass_utils import run_bass_kernel_spmd

    x, adj = np.asarray(x), np.asarray(adj)
    x_tok = x.reshape(NG, G, S, H).transpose(0, 2, 1, 3)
    x_feat = x.reshape(NG, G, S, HC, P).transpose(0, 4, 3, 1, 2).reshape(NG, P, HC, TOK)
    adj_tok = adj.reshape(NG, G, S, S).transpose(0, 2, 1, 3)
    adj_t = adj.reshape(NG, G, S, S).transpose(0, 3, 1, 2)
    w = np.stack([np.asarray(a) for a in (L0_gnn_W_left, L0_gnn_W_right, L0_gnn_W_lin)], axis=1)
    w_feat = w.reshape(L, 3, H, HC, P).transpose(0, 1, 4, 3, 2)
    arrays = {
        "x_tok": x_tok, "x_feat": x_feat, "adj_pair": np.stack([adj_tok, adj_t], axis=2),
        "w_feat": w_feat, "b_lin": L0_gnn_b_lin, "ln_a": L0_gnn_ln_a, "ln_b": L0_gnn_ln_b,
        "identity_in": np.eye(S, dtype=np.float32),
        "triangles_in": np.stack([np.triu(np.ones((S, S), np.float32)),
                                  np.tril(np.ones((S, S), np.float32), -1)], axis=1),
    }
    nc = bacc.Bacc("TRN2", target_bir_lowering=False, num_devices=1)
    in_map, args = {}, []
    for name, a in arrays.items():
        a = np.ascontiguousarray(a)
        in_map[name + "_dram"] = a
        args.append(nc.dram_tensor(name + "_dram", a.shape, F32, kind="ExternalInput").ap())
    out = nc.dram_tensor("out_dram", (NG, S, G, H), F32, kind="ExternalOutput").ap()
    build(nc, *args, out)
    r = run_bass_kernel_spmd(nc, [in_map], core_ids=[0])
    got = r.results[0]["out_dram"]
    return np.ascontiguousarray(got.transpose(0, 2, 1, 3).reshape(B, S, H))
```

```python
from contextlib import ExitStack

import concourse.bass as bass
from concourse import mybir

F32 = mybir.dt.float32
F32R = mybir.dt.float32r
ALU = mybir.AluOpType
ACT = mybir.ActivationFunctionType
AX = mybir.AxisListType

B, S, H, L = 64, 128, 384, 2
P = 128
G = 512 // S
NG = B // G
HC = H // P
TOK = G * S
TEMPER = float(H) ** 0.5
LN_EPS = 1e-3
SUM_EPS = 1e-10
OUT_EPS = 1e-5
M_TILES = 2 * HC
UNIT_TILES = M_TILES + G
LEFT, RIGHT, LIN = range(3)
DMA = 16


class Slot:

    def __init__(self, n, tile0, layer, prev_layer=None, prev_group=None, prev_mask=None, transposes=None,
                 late_transposes=None, mask_group=None, mask_buf=None, split_group=None,
                 final=None, final_buf=None, parity=0, hurried=False, early=False,
                 group=None, mask=None):
        self.n = n
        self.at = n if isinstance(n, int) else None
        self.tile0 = tile0
        self.layer = layer
        self.prev_layer = prev_layer
        self.prev_group = prev_group
        self.prev_mask = prev_mask
        self.transposes = transposes
        self.late = late_transposes
        self.mask_group = mask_group
        self.mask_buf = mask_buf
        self.split_group = split_group
        self.final = final
        self.final_buf = final_buf
        self.parity = parity
        self.hurried = hurried
        self.early = early
        self.group = group
        self.mask = mask


PAIR_TILES = 2 * UNIT_TILES + HC
PAIRS = NG - 1
UNITS = NG * L


def odd_slot(k, k_parity, first=False):
    return Slot(2 * k + 1, PAIR_TILES * k + UNIT_TILES, 0,
                prev_layer=0 if first else 1, prev_group=0 if first else k - 1,
                prev_mask=0 if first else 1 - k_parity,
                transposes=None if first else k,
                mask_group=k + 1, mask_buf=1 - k_parity, parity=1,
                hurried=first, early=first, group=k + 1, mask=1 - k_parity)


def even_slot(k, k_parity, first=False, last=False):
    return Slot(2 * k + 2, PAIR_TILES * k + 2 * UNIT_TILES + HC, 1,
                prev_layer=0, prev_group=k + 1, prev_mask=1 - k_parity, late_transposes=0 if first else None,
                split_group=None if last else k + 2,
                final=None if first else k - 1, final_buf=None if first else 1 - k_parity,
                parity=0, hurried=last, early=last, group=k, mask=k_parity)


LOOPS = (PAIRS - 3) // 2
assert PAIRS == 3 + 2 * LOOPS


def head_slots():
    return [Slot(0, 0, 0, split_group=1, parity=0),
            odd_slot(0, 0, first=True), even_slot(0, 0, first=True),
            odd_slot(1, 1), even_slot(1, 1)]


def loop_slots(r):
    return [odd_slot(2 * r + 2, 0), even_slot(2 * r + 2, 0),
            odd_slot(2 * r + 3, 1), even_slot(2 * r + 3, 1)]


def tail_slots():
    k = PAIRS - 1
    return [odd_slot(k, k % 2), even_slot(k, k % 2, last=True),
            Slot(UNITS - 1, PAIR_TILES * PAIRS + UNIT_TILES + HC, 1, prev_layer=1,
                 prev_group=NG - 2, prev_mask=(NG - 2) % 2, late_transposes=PAIRS, parity=(UNITS - 1) % 2,
                 early=True, group=NG - 1, mask=(NG - 1) % 2,
                 final=NG - 2, final_buf=(NG - 2) % 2)]


def drained_before(slot, t):
    return slot.tile0 + (t - 2 if t >= 3 else (0, -2, -1)[t])


def build(nc, x_tok, x_feat, adj_pair, w_feat, b_lin, ln_a, ln_b, identity_in, triangles_in, out):
    ctx = ExitStack()
    with ctx:
        def sb(name, shape, dt=F32):
            return ctx.enter_context(nc.sbuf_tensor(name, shape, dt))

        def psum(name, shape):
            return ctx.enter_context(nc.psum_tensor(name, shape, F32))

        def sem(name):
            return ctx.enter_context(nc.semaphore(name))

        identity = sb("identity", [P, S])
        triangles = sb("triangles", [P, 2, S])
        bias = sb("bias", [P, L, H])
        gain = sb("gain", [P, L, H])
        offset = sb("offset", [P, L, H])
        half = sb("half", [P, G])
        minus_half = sb("minus_half", [P, G])
        unbiased = sb("unbiased", [P, G])
        out_eps = sb("out_eps", [P, G])
        w_hi = sb("w_hi", [P, L, 3, HC, H], F32R)
        w_lo = sb("w_lo", [P, L, 3, HC, H], F32R)
        x_in = sb("x_in", [P, HC, TOK])
        adj = [sb(f"adj{i}", [P, 2, G, S]) for i in range(2)]
        gate = [sb(f"gate{i}", [P, 2, G, S]) for i in range(2)]
        residual = [sb(f"residual{i}", [P, G, H]) for i in range(2)]
        ht_hi = [sb(f"ht_hi{i}", [P, HC, TOK], F32R) for i in range(2)]
        ht_lo = [sb(f"ht_lo{i}", [P, HC, TOK], F32R) for i in range(2)]
        m_hi = sb("m_hi", [P, HC, 2, TOK], F32R)
        m_lo = sb("m_lo", [P, HC, 2, TOK], F32R)
        hlin = sb("hlin", [P, G, H])
        hlin_hi = sb("hlin_hi", [P, G, H], F32R)
        hlin_lo = sb("hlin_lo", [P, G, H], F32R)
        gated = sb("gated", [P, 2, G, S])
        score = sb("score", [P, G, S])
        expd = sb("expd", [P, G, S])
        delta = sb("delta", [P, G, S])
        att_hi = sb("att_hi", [P, TOK], F32R)
        att_lo = sb("att_lo", [P, TOK], F32R)
        row_sum = sb("row_sum", [P, G])
        row_den = sb("row_den", [P, G])
        row_scale = sb("row_scale", [P, G])
        z = sb("z", [P, G, H])
        stats = sb("stats", [P, G, 6])
        moments = sb("moments", [P, G, 2])
        variance = sb("variance", [P, G])
        sigma = sb("sigma", [P, G])
        ln_den = sb("ln_den", [P, G])
        ln_scale = sb("ln_scale", [P, G])
        ln_shift = sb("ln_shift", [P, G])
        h1 = sb("h1", [P, G, H])
        h2 = sb("h2", [P, G, H])
        out_stats = sb("out_stats", [P, G, 6])
        out_moments = sb("out_moments", [P, G, 2])
        out_var = sb("out_var", [P, G])
        out_scale = sb("out_scale", [P, G])
        out_shift = sb("out_shift", [P, G])
        result = sb("result", [P, G, H])
        raw_w = [[b[:].rearrange("p b h -> p (b h)")[:, 0:HC * H].rearrange("p (c o) -> p c o", c=HC)
                  for b in bufs] for bufs in ((z, h1, h2), (residual[0], residual[1], result))]

        tile = [psum(f"tile{i}", [P, TOK]) for i in range(3)]
        u_bank = [psum(f"u_bank{i}", [P, 2, 2, S]) for i in range(2)]
        att_bank = psum("att_bank", [P, TOK])
        c_bank = [psum(f"c_bank{i}", [P, H]) for i in range(2)]

        w_in = [[sem(f"w_in{l}{k}") for k in range(3)] for l in range(L)]
        consts_in = sem("consts_in")
        x0_landed = [sem(f"x0_landed{c}") for c in range(HC)]
        x_landed = sem("x_landed")
        wl_landed = [sem(f"wl_landed{c}") for c in range(HC)]
        adj_landed = sem("adj_landed")
        residual_landed = [sem(f"residual_landed{i}") for i in range(2)]
        stored = sem("stored")
        tile_full = sem("tile_full")
        u_full = sem("u_full")
        att_full = sem("att_full")
        c_full = sem("c_full")
        w_hi0_done = sem("w_hi0_done")
        w_hi1_done = sem("w_hi1_done")
        m_hi_done = sem("m_hi_done")
        hlin_hi_done = sem("hlin_hi_done")
        ht_hi_done = sem("ht_hi_done")
        exp_done = sem("exp_done")
        att_hi_done = sem("att_hi_done")
        z_done = sem("z_done")
        norm_done = sem("norm_done")
        tile_drained = sem("tile_drained")
        w_lo0_done = sem("w_lo0_done")
        x_hi0_done = sem("x_hi0_done")
        x_hi_done = sem("x_hi_done")
        gated_done = sem("gated_done")
        score_done = sem("score_done")
        delta_done = sem("delta_done")
        row_sum_done = sem("row_sum_done")
        row_den_done = sem("row_den_done")
        row_scale_done = sem("row_scale_done")
        att_lo_done = sem("att_lo_done")
        stats_done = sem("stats_done")
        moments_done = sem("moments_done")
        ln_den_done = sem("ln_den_done")
        ln_scale_done = sem("ln_scale_done")
        ln_shift_done = sem("ln_shift_done")
        summed_done = sem("summed_done")
        out_stats_done = sem("out_stats_done")
        out_moments_done = sem("out_moments_done")
        result_done = sem("result_done")
        last_h_done = sem("last_h_done")
        x_lo0_done = sem("x_lo0_done")
        scalars_set = sem("scalars_set")
        w_lo1_done = sem("w_lo1_done")
        x_lo_done = sem("x_lo_done")
        gate_done = sem("gate_done")
        hlin_lo_done = sem("hlin_lo_done")
        variance_done = sem("variance_done")
        sigma_done = sem("sigma_done")
        gained_done = sem("gained_done")
        h_done = sem("h_done")
        out_var_done = sem("out_var_done")
        out_scale_done = sem("out_scale_done")
        out_shift_done = sem("out_shift_done")

        block = ctx.enter_context(nc.Block())

        def chunk(b):
            return slice(b * S, (b + 1) * S)

        @block.sync
        def _(sp):
            for c in range(HC):
                sp.dma_start(x_in[:, c], x_feat[0, :, c]).then_inc(x0_landed[c], DMA)
                sp.dma_start(raw_w[0][LEFT][:, c], w_feat[0, LEFT, :, c]).then_inc(wl_landed[c], DMA)
            sp.dma_start(raw_w[0][RIGHT], w_feat[0, RIGHT]).then_inc(w_in[0][RIGHT], DMA)
            sp.dma_start(raw_w[0][LIN], w_feat[0, LIN]).then_inc(w_in[0][LIN], DMA)
            sp.dma_start(bias[:], b_lin.partition_broadcast(P)).then_inc(consts_in, DMA)
            sp.dma_start(identity[:], identity_in).then_inc(consts_in, DMA)
            sp.dma_start(triangles[:], triangles_in).then_inc(consts_in, DMA)
            sp.dma_start(gain[:], ln_a.partition_broadcast(P)).then_inc(consts_in, DMA)
            sp.dma_start(offset[:], ln_b.partition_broadcast(P)).then_inc(consts_in, DMA)
            sp.dma_start(adj[0][:], adj_pair[0]).then_inc(adj_landed, DMA)
            sp.wait_ge(x_lo0_done, HC)
            sp.dma_start(x_in[:], x_feat[1]).then_inc(x_landed, DMA)
            for kind in range(3):
                sp.dma_start(raw_w[1][kind], w_feat[1, kind]).then_inc(w_in[1][kind], DMA)
            sp.wait_ge(adj_landed, DMA)
            sp.dma_start(adj[1][:], adj_pair[1]).then_inc(adj_landed, DMA)

            def load_x(k):
                sp.wait_ge(x_lo_done, k + 1)
                sp.dma_start(x_in[:], x_feat[k + 2]).then_inc(x_landed, DMA)

            def load_adj(k, k_parity):
                sp.wait_ge(delta_done, 2 * k + 1)
                sp.dma_start(adj[1 - k_parity][:], adj_pair[k + 1]).then_inc(adj_landed, DMA)

            def load_residual(g, g_parity):
                sp.dma_start(residual[g_parity][:], x_tok[g]).then_inc(residual_landed[g_parity], DMA)

            def store(g):
                sp.wait_ge(result_done, G * (g + 1))
                sp.dma_start(out[g], result[:]).then_inc(stored, DMA)

            def pair(k, k_parity):
                load_x(k)
                load_adj(k, k_parity)
                load_residual(k, k_parity)
                store(k - 1)

            load_x(0)
            sp.wait_ge(w_lo1_done, 3)
            load_residual(0, 0)
            pair(1, 1)
            with sp.Fori(0, LOOPS) as r:
                pair(2 * r + 2, 0)
                pair(2 * r + 3, 1)
            k = PAIRS - 1
            load_adj(k, k % 2)
            load_residual(k, k % 2)
            store(k - 1)
            load_residual(NG - 1, (NG - 1) % 2)
            store(NG - 2)
            for b in range(G):
                sp.wait_ge(result_done, G * (NG - 1) + b + 1)
                sp.dma_start(out[NG - 1, :, b], result[:, b]).then_inc(stored, DMA)
            sp.wait_ge(stored, DMA * (NG - 1 + G))

        @block.tensor
        def _(pe):
            def passes(dst, lhs_hi, lhs_lo, rhs_hi, rhs_lo, first, last):
                nc.tensor.matmul(dst, lhs_hi, rhs_hi, start=first, stop=False)
                nc.tensor.matmul(dst, lhs_hi, rhs_lo, start=False, stop=False)
                return nc.tensor.matmul(dst, lhs_lo, rhs_hi, start=False, stop=last)

            def transpose_attention(n):
                pe.wait_ge(delta_done, n + 1)
                if isinstance(n, int) and n == 0:
                    pe.wait_ge(consts_in, 5 * DMA)
                else:
                    pe.wait_ge(att_lo_done, n)
                for b in range(G):
                    last = nc.tensor.transpose(att_bank[:, chunk(b)], delta[:, b, :], identity[:])
                last.then_inc(att_full, 1)

            def context(n, b):
                if b == 0:
                    pe.wait_ge(att_lo_done, n + 1)
                pe.wait_ge(hlin_lo_done, G * n + b + 1)
                if b >= 2 or not isinstance(n, int) or n > 0:
                    pe.wait_ge(z_done, G * n + b - 1)
                passes(c_bank[b % 2][:], att_hi[:, chunk(b)], att_lo[:, chunk(b)],
                       hlin_hi[:, b, :], hlin_lo[:, b, :], True, True).then_inc(c_full, 1)

            def slot(s):
                hi, lo = ht_hi[s.parity], ht_lo[s.parity]
                prev = s.prev_layer is not None

                def project(t):
                    side, oc = t // HC, t % HC
                    if t >= 3 or s.at != 0:
                        pe.wait_ge(tile_drained, drained_before(s, t))
                    if s.at == 0 and t == HC:
                        pe.wait_ge(w_lo0_done, HC + 1)
                    for hc in range(HC):
                        if s.at == 0 and t == 0:
                            pe.wait_ge(x_lo0_done, hc + 1)
                            pe.wait_ge(w_lo0_done, hc + 1)
                        last = passes(tile[t % 3][:],
                                      w_hi[:, s.layer, side, hc, chunk(oc)],
                                      w_lo[:, s.layer, side, hc, chunk(oc)],
                                      hi[:, hc, :], lo[:, hc, :], hc == 0, hc == HC - 1)
                    last.then_inc(tile_full, 1)

                def linear(b):
                    t = M_TILES + b
                    pe.wait_ge(tile_drained, drained_before(s, t))
                    if s.at == 0 and b == 0:
                        pe.wait_ge(w_lo0_done, HC + 2)
                    for hc in range(HC):
                        last = passes(tile[t % 3][:, 0:H], hi[:, hc, chunk(b)], lo[:, hc, chunk(b)],
                                      w_hi[:, s.layer, LIN, hc, :], w_lo[:, s.layer, LIN, hc, :],
                                      hc == 0, hc == HC - 1)
                    last.then_inc(tile_full, 1)

                def transpose_h(hc, tile0, h_count):
                    if hc == 0:
                        pe.wait_ge(h_done, h_count)
                    t = UNIT_TILES + hc
                    pe.wait_ge(tile_drained, tile0 + t - 2)
                    for b in range(G):
                        last = nc.tensor.transpose(tile[t % 3][:, chunk(b)], h1[:, b, chunk(hc)],
                                                   identity[:])
                    last.then_inc(tile_full, 1)

                def scores(b):
                    if b == 0:
                        pe.wait_ge(tile_drained, s.tile0 + M_TILES)
                    if b % 2 == 0 and s.at != 0:
                        pe.wait_ge(gated_done, 2 * (s.n - 1) + b // 2 + 1)
                    for hc in range(HC):
                        last = passes(u_bank[b // 2][:, b % 2, :, :], hi[:, hc, chunk(b)], lo[:, hc, chunk(b)],
                                      m_hi[:, hc, :, chunk(b)], m_lo[:, hc, :, chunk(b)],
                                      hc == 0, hc == HC - 1)
                    if b % 2 == 1:
                        last.then_inc(u_full, 1)

                if s.late is not None:
                    transpose_attention(s.n - 1)
                    for hc in range(HC):
                        transpose_h(hc, s.tile0 - HC - UNIT_TILES, s.n - 1)
                    for b in range(G):
                        context(s.n - 1, b)
                    pe.wait_ge(tile_drained, s.tile0)
                    if s.n == 2:
                        pe.wait_ge(w_lo1_done, 3)
                    for t in range(M_TILES):
                        project(t)
                    for b in range(2 if s.early else G):
                        linear(b)
                elif s.hurried:
                    if s.layer == 0:
                        pe.wait_ge(x_lo_done, s.mask_group)
                    project(0)
                    project(1)
                    transpose_attention(s.n - 1)
                    project(2)
                    project(3)
                    for b in range(G):
                        context(s.n - 1, b)
                    project(4)
                    project(5)
                    linear(0)
                    linear(1)
                else:
                    if s.layer == 0 and s.at != 0:
                        pe.wait_ge(x_lo_done, s.mask_group)
                    for t in range(HC):
                        project(t)
                    if prev:
                        transpose_attention(s.n - 1)
                    for t in range(HC, M_TILES):
                        project(t)
                    if prev:
                        context(s.n - 1, 0)
                        context(s.n - 1, 1)
                    linear(0)
                    if prev:
                        context(s.n - 1, 2)
                        context(s.n - 1, 3)
                    for b in range(1, G):
                        linear(b)
                if s.transposes is not None:
                    transpose_h(0, s.tile0, s.n - 1)
                    transpose_h(1, s.tile0, s.n - 1)
                scores(0)
                if s.transposes is not None:
                    transpose_h(2, s.tile0, s.n - 1)
                for b in range(1, G):
                    scores(b)
                if s.early:
                    linear(2)
                    linear(3)

            for s in head_slots():
                slot(s)
            with pe.Fori(0, LOOPS) as r:
                for s in loop_slots(r):
                    slot(s)
            for s in tail_slots():
                slot(s)
            transpose_attention(UNITS - 1)
            for b in range(G):
                context(UNITS - 1, b)

        @block.scalar
        def _(act):
            def exponent(n):
                act.wait_ge(score_done, n + 1)
                nc.scalar.activation(expd[:], score[:], ACT.Exp, scale=1.0 / TEMPER).then_inc(exp_done, 1)

            def attention_high(n):
                act.wait_ge(att_full, n + 1)
                nc.scalar.activation(att_hi[:], att_bank[:], ACT.Copy).then_inc(att_hi_done, 1)

            def context_out(n, b):
                if b == 0:
                    act.wait_ge(row_scale_done, n + 1)
                    if not isinstance(n, int) or n > 0:
                        act.wait_ge(h_done, n)
                act.wait_ge(c_full, G * n + b + 1)
                nc.scalar.activation(z[:, b, :], c_bank[b % 2][:], ACT.Copy,
                                     scale=row_scale[:, b:b + 1]).then_inc(z_done, 1)

            def normalise(n):
                act.wait_ge(ln_shift_done, n + 1)
                for b in range(G):
                    nc.scalar.activation(z[:, b, :], z[:, b, :], ACT.Identity, bias=ln_shift[:, b:b + 1],
                                         scale=ln_scale[:, b:b + 1]).then_inc(norm_done, 1)

            def slot(s):
                prev = s.prev_layer is not None

                def m_high(t):
                    act.wait_ge(tile_full, s.tile0 + t + 1)
                    nc.scalar.activation(m_hi[:, t % HC, t // HC, :], tile[t % 3][:], ACT.Copy)\
                      .then_inc(m_hi_done, 1)

                def hlin_high(b):
                    act.wait_ge(tile_drained, s.tile0 + M_TILES + b + 1)
                    nc.scalar.activation(hlin_hi[:, b, :], hlin[:, b, :], ACT.Copy)\
                      .then_inc(hlin_hi_done, 1)

                def h_high(hc, tile0, buf):
                    act.wait_ge(tile_full, tile0 + UNIT_TILES + hc + 1)
                    nc.scalar.activation(ht_hi[buf][:, hc, :], tile[(UNIT_TILES + hc) % 3][:], ACT.Relu)\
                      .then_inc(ht_hi_done, 1)

                if prev and s.late is None:
                    exponent(s.n - 1)
                if s.late is not None:
                    attention_high(s.n - 1)
                    for hc in range(HC):
                        h_high(hc, s.tile0 - HC - UNIT_TILES, s.parity)
                    for b in range(G):
                        context_out(s.n - 1, b)
                    m_high(0)
                    m_high(1)
                    normalise(s.n - 1)
                    for t in range(2, M_TILES):
                        m_high(t)
                    hlin_high(0)
                    hlin_high(1)
                elif s.hurried:
                    m_high(0)
                    m_high(1)
                    attention_high(s.n - 1)
                    m_high(2)
                    m_high(3)
                    for b in range(G):
                        context_out(s.n - 1, b)
                    m_high(4)
                    m_high(5)
                    normalise(s.n - 1)
                    hlin_high(0)
                    hlin_high(1)
                else:
                    for t in range(HC):
                        m_high(t)
                    if prev:
                        attention_high(s.n - 1)
                    for t in range(HC, M_TILES):
                        m_high(t)
                    if prev:
                        context_out(s.n - 1, 0)
                        context_out(s.n - 1, 1)
                    hlin_high(0)
                    if prev:
                        context_out(s.n - 1, 2)
                        context_out(s.n - 1, 3)
                    hlin_high(1)
                    hlin_high(2)
                    if s.transposes is not None:
                        h_high(0, s.tile0, 1 - s.parity)
                        h_high(1, s.tile0, 1 - s.parity)
                    hlin_high(3)
                    if s.transposes is not None:
                        h_high(2, s.tile0, 1 - s.parity)
                    if prev:
                        normalise(s.n - 1)
                if s.early:
                    exponent(s.n)
                    hlin_high(2)
                    hlin_high(3)
                elif s.late is not None:
                    hlin_high(2)
                    hlin_high(3)

            for c in range(HC):
                act.wait_ge(wl_landed[c], DMA)
                nc.scalar.activation(w_hi[:, 0, LEFT, c], raw_w[0][LEFT][:, c], ACT.Copy)\
                  .then_inc(w_hi0_done, 1)
            for kind in (RIGHT, LIN):
                act.wait_ge(w_in[0][kind], DMA)
                nc.scalar.activation(w_hi[:, 0, kind], raw_w[0][kind], ACT.Copy).then_inc(w_hi0_done, 1)
            head = head_slots()
            slot(head[0])
            for kind in range(3):
                act.wait_ge(w_in[1][kind], DMA)
                nc.scalar.activation(w_hi[:, 1, kind], raw_w[1][kind], ACT.Copy).then_inc(w_hi1_done, 1)
            for s in head[1:]:
                slot(s)
            with act.Fori(0, LOOPS) as r:
                for s in loop_slots(r):
                    slot(s)
            for s in tail_slots():
                slot(s)
            attention_high(UNITS - 1)
            for b in range(G):
                context_out(UNITS - 1, b)
            g, buf = NG - 2, (NG - 2) % 2
            act.wait_ge(out_shift_done, 1)
            act.wait_ge(stored, DMA * g)
            for b in range(G):
                nc.scalar.activation(result[:, b], residual[buf][:, b], ACT.Identity,
                                     bias=out_shift[:, b:b + 1], scale=out_scale[:, b:b + 1])\
                  .then_inc(result_done, 1)

        @block.vector
        def _(dve):
            def gate_scores(n, group, buf):
                dve.wait_ge(gate_done, group + 1)
                for k in range(2):
                    dve.wait_ge(u_full, 2 * n + k + 1)
                    nc.vector.tensor_tensor(
                        gated[:, :, 2 * k:2 * k + 2, :], u_bank[k][:].rearrange("p b s j -> p s b j"),
                        gate[buf][:, :, 2 * k:2 * k + 2, :], ALU.mult).then_inc(gated_done, 1)
                dve.wait_ge(gated_done, 2 * (n + 1))
                nc.vector.tensor_tensor(score[:], gated[:, 0], gated[:, 1], ALU.add)\
                  .then_inc(score_done, 1)

            def attend(n, buf):
                dve.wait_ge(exp_done, n + 1)
                nc.vector.tensor_tensor(delta[:], expd[:], adj[buf][:, 0], ALU.mult)\
                  .then_inc(delta_done, 1)

            def row_scales(n):
                dve.wait_ge(delta_done, n + 1)
                nc.vector.reduce_sum(row_sum[:], delta[:], AX.X).then_inc(row_sum_done, 1)
                dve.wait_ge(row_sum_done, n + 1)
                nc.vector.tensor_scalar(row_den[:], row_sum[:], SUM_EPS, None, ALU.add)\
                  .then_inc(row_den_done, 1)
                dve.wait_ge(row_den_done, n + 1)
                nc.vector.reciprocal(row_scale[:], row_den[:]).then_inc(row_scale_done, 1)

            def attention_low(n):
                dve.wait_ge(att_hi_done, n + 1)
                nc.vector.tensor_tensor(att_lo[:], att_bank[:], att_hi[:].bitcast(F32), ALU.subtract)\
                  .then_inc(att_lo_done, 1)

            def ln_stats(n, batches):
                for b in batches:
                    dve.wait_ge(z_done, G * n + b + 1)
                    nc.vector.bn_stats(stats[:, b, :], z[:, b, :]).then_inc(stats_done, 1)

            def ln_moments():
                for b in range(G):
                    last = nc.vector.bn_aggr(moments[:, b, :], stats[:, b, :])
                last.then_inc(moments_done, 1)

            def ln_scales(n):
                dve.wait_ge(sigma_done, n + 1)
                nc.vector.tensor_scalar(ln_den[:], sigma[:], LN_EPS, None, ALU.add)\
                  .then_inc(ln_den_done, 1)
                dve.wait_ge(ln_den_done, n + 1)
                nc.vector.reciprocal(ln_scale[:], ln_den[:]).then_inc(ln_scale_done, 1)
                dve.wait_ge(ln_scale_done, n + 1)
                nc.vector.scalar_tensor_tensor(out=ln_shift[:], in0=moments[:, :, 0], scalar=-1.0,
                                               in1=ln_scale[:], op0=ALU.mult, op1=ALU.mult)\
                  .then_inc(ln_shift_done, 1)

            def out_sum(g, buf, b):
                nc.vector.scalar_tensor_tensor(out=residual[buf][:, b], in0=h2[:, b], scalar=0.0,
                                               in1=residual[buf][:, b], op0=ALU.max, op1=ALU.add)\
                  .then_inc(summed_done, 1)

            def residual_ready(g, buf):
                dve.wait_ge(residual_landed[buf], DMA // 2 * (g - buf) + DMA)

            def out_statistics(g, buf, b):
                dve.wait_ge(summed_done, G * g + b + 1)
                nc.vector.bn_stats(out_stats[:, b, :], residual[buf][:, b, :])\
                  .then_inc(out_stats_done, 1)

            def out_aggregate():
                for b in range(G):
                    last = nc.vector.bn_aggr(out_moments[:, b, :], out_stats[:, b, :])
                last.then_inc(out_moments_done, 1)

            def out_normalise(g, buf):
                dve.wait_ge(out_scale_done, g + 1)
                if not isinstance(g, int) or g > 0:
                    dve.wait_ge(stored, DMA * g)
                for b in range(G):
                    nc.vector.tensor_scalar(result[:, b, :], residual[buf][:, b, :],
                                            out_moments[:, b, 0:1], out_scale[:, b:b + 1],
                                            ALU.subtract, ALU.mult).then_inc(result_done, 1)

            def slot(s):
                prev, final = s.prev_layer is not None, s.final is not None

                def m_low(t):
                    dve.wait_ge(m_hi_done, M_TILES * s.n + t + 1)
                    nc.vector.tensor_tensor(m_lo[:, t % HC, t // HC, :], tile[t % 3][:],
                                            m_hi[:, t % HC, t // HC, :].bitcast(F32), ALU.subtract)\
                      .then_inc(tile_drained, 1)

                def x_high():
                    dve.wait_ge(x_landed, DMA * s.split_group)
                    nc.vector.tensor_copy(ht_hi[1 - s.parity][:], x_in[:]).then_inc(x_hi_done, 1)

                def h_low(hc, buf, second):
                    dve.wait_ge(ht_hi_done, HC * second + hc + 1)
                    nc.vector.scalar_tensor_tensor(
                        out=ht_lo[buf][:, hc, :], in0=tile[(UNIT_TILES + hc) % 3][:], scalar=0.0,
                        in1=ht_hi[buf][:, hc, :].bitcast(F32), op0=ALU.max, op1=ALU.subtract)\
                      .then_inc(tile_drained, 1)

                def hlin_bias(b):
                    dve.wait_ge(tile_full, s.tile0 + M_TILES + b + 1)
                    if s.at == 0 and b == 0:
                        dve.wait_ge(consts_in, 5 * DMA)
                    elif s.at != 0:
                        dve.wait_ge(hlin_lo_done, G * (s.n - 1) + b + 1)
                    nc.vector.tensor_tensor(hlin[:, b, :], tile[(M_TILES + b) % 3][:, 0:H],
                                            bias[:, s.layer, :], ALU.add).then_inc(tile_drained, 1)

                def final_sum(h_count):
                    dve.wait_ge(h_done, h_count)
                    residual_ready(s.final, s.final_buf)
                    for b in range(G):
                        out_sum(s.final, s.final_buf, b)

                def final_moments():
                    for b in range(G):
                        out_statistics(s.final, s.final_buf, b)
                    dve.wait_ge(out_stats_done, G * (s.final + 1))
                    out_aggregate()

                def w_low(kind):
                    dve.wait_ge(w_hi0_done, HC + kind)
                    nc.vector.tensor_tensor(w_lo[:, 0, kind], raw_w[0][kind], w_hi[:, 0, kind].bitcast(F32),
                                            ALU.subtract).then_inc(w_lo0_done, 1)

                def early_softmax():
                    gate_scores(s.n, s.group, s.mask)
                    hlin_bias(2)
                    attend(s.n, s.mask)
                    hlin_bias(3)

                if prev and s.late is None:
                    gate_scores(s.n - 1, s.prev_group, s.prev_mask)
                    attend(s.n - 1, s.prev_mask)
                if s.hurried:
                    m_low(0)
                    row_scales(s.n - 1)
                    m_low(1)
                    attention_low(s.n - 1)
                    m_low(2)
                    m_low(3)
                    ln_stats(s.n - 1, range(G))
                    dve.wait_ge(stats_done, G * s.n)
                    ln_moments()
                    m_low(4)
                    ln_scales(s.n - 1)
                    m_low(5)
                    if s.final is not None:
                        final_sum(s.n - 1)
                        final_moments()
                    hlin_bias(0)
                    hlin_bias(1)
                    early_softmax()
                    if s.final is not None:
                        out_normalise(s.final, s.final_buf)
                    return
                if s.late is not None:
                    row_scales(s.n - 1)
                    attention_low(s.n - 1)
                    for hc in range(HC):
                        h_low(hc, s.parity, s.late)
                    ln_stats(s.n - 1, range(G))
                    dve.wait_ge(stats_done, G * s.n)
                    ln_moments()
                    m_low(0)
                    m_low(1)
                    ln_scales(s.n - 1)
                    for t in range(2, M_TILES):
                        m_low(t)
                    if s.split_group is not None:
                        x_high()
                    hlin_bias(0)
                    hlin_bias(1)
                    if final:
                        final_sum(s.n)
                    if s.early:
                        early_softmax()
                    else:
                        hlin_bias(2)
                        hlin_bias(3)
                    return
                m_low(0)
                if s.at == 0:
                    w_low(RIGHT)
                if s.split_group is not None and s.at != 0:
                    x_high()
                m_low(1)
                if prev:
                    row_scales(s.n - 1)
                if final:
                    final_sum(s.n - 1)
                m_low(2)
                if s.at == 0:
                    w_low(LIN)
                if prev:
                    attention_low(s.n - 1)
                if final:
                    for b in range(G):
                        out_statistics(s.final, s.final_buf, b)
                    dve.wait_ge(out_stats_done, G * (s.final + 1))
                m_low(3)
                if final:
                    out_aggregate()
                m_low(4)
                m_low(5)
                if s.at == 0:
                    x_high()
                if final:
                    out_normalise(s.final, s.final_buf)
                if prev:
                    ln_stats(s.n - 1, (0, 1))
                hlin_bias(0)
                if prev:
                    ln_stats(s.n - 1, (2, 3))
                    dve.wait_ge(stats_done, G * s.n)
                hlin_bias(1)
                if prev:
                    ln_moments()
                hlin_bias(2)
                if prev:
                    ln_scales(s.n - 1)
                hlin_bias(3)
                if s.transposes is not None:
                    for hc in range(HC):
                        h_low(hc, 1 - s.parity, s.transposes)

            for c in range(HC):
                dve.wait_ge(x0_landed[c], DMA)
                nc.vector.tensor_copy(ht_hi[0][:, c], x_in[:, c]).then_inc(x_hi0_done, 1)
                dve.wait_ge(x_hi0_done, c + 1)
                nc.vector.tensor_tensor(ht_lo[0][:, c], x_in[:, c], ht_hi[0][:, c].bitcast(F32),
                                        ALU.subtract).then_inc(x_lo0_done, 1)
                dve.wait_ge(w_hi0_done, c + 1)
                nc.vector.tensor_tensor(w_lo[:, 0, LEFT, c], raw_w[0][LEFT][:, c],
                                        w_hi[:, 0, LEFT, c].bitcast(F32), ALU.subtract)\
                  .then_inc(w_lo0_done, 1)
            for s in head_slots():
                slot(s)
            with dve.Fori(0, LOOPS) as r:
                for s in loop_slots(r):
                    slot(s)
            for s in tail_slots():
                slot(s)

            n, g = UNITS - 1, NG - 1
            row_scales(n)
            attention_low(n)
            for b in range(G):
                out_statistics(g - 1, (g - 1) % 2, b)
            dve.wait_ge(out_stats_done, G * g)
            out_aggregate()
            ln_stats(n, range(G))
            dve.wait_ge(stats_done, G * (n + 1))
            ln_moments()
            dve.wait_ge(out_scale_done, g)
            nc.vector.scalar_tensor_tensor(out=out_shift[:], in0=out_moments[:, :, 0], scalar=-1.0,
                                           in1=out_scale[:], op0=ALU.mult, op1=ALU.mult)\
              .then_inc(out_shift_done, 1)
            dve.wait_ge(moments_done, n + 1)
            for b in range(G):
                nc.vector.scalar_tensor_tensor(out=z[:, b], in0=z[:, b], scalar=moments[:, b, 0:1],
                                               in1=gain[:, 1], op0=ALU.subtract, op1=ALU.mult)\
                  .then_inc(gained_done, 1)
            ln_scales(n)
            residual_ready(g, g % 2)
            dve.wait_ge(summed_done, G * g)
            dve.wait_ge(ln_scale_done, n + 1)
            for step in range(G + 2):
                if step < G:
                    dve.wait_ge(gained_done, G * n + step + 1)
                    nc.vector.scalar_tensor_tensor(out=h2[:, step], in0=z[:, step],
                                                   scalar=ln_scale[:, step:step + 1],
                                                   in1=offset[:, 1], op0=ALU.mult, op1=ALU.add)\
                      .then_inc(last_h_done, 1)
                if 1 <= step <= G:
                    dve.wait_ge(last_h_done, step)
                    out_sum(g, g % 2, step - 1)
                if step >= 2:
                    out_statistics(g, g % 2, step - 2)
            dve.wait_ge(out_stats_done, G * (g + 1))
            dve.wait_ge(result_done, G * g)
            out_aggregate()
            out_normalise(g, g % 2)

        @block.gpsimd
        def _(pool):
            def mask(group, buf):
                pool.wait_ge(adj_landed, DMA * (group + 1))
                nc.gpsimd.tensor_tensor(gate[buf][:], adj[buf][:],
                                        triangles[:].unsqueeze(2).to_broadcast([P, 2, G, S]),
                                        ALU.mult).then_inc(gate_done, 1)

            def ln_sigma(n):
                pool.wait_ge(moments_done, n + 1)
                nc.gpsimd.tensor_tensor(variance[:], moments[:, :, 1], unbiased[:], ALU.mult)\
                  .then_inc(variance_done, 1)
                pool.wait_ge(variance_done, n + 1)
                nc.gpsimd.tensor_tensor(sigma[:], variance[:], half[:], ALU.pow).then_inc(sigma_done, 1)

            def ln_gain(n, layer):
                for b in range(G):
                    pool.wait_ge(norm_done, G * n + b + 1)
                    nc.gpsimd.tensor_tensor(z[:, b], z[:, b], gain[:, layer], ALU.mult)\
                      .then_inc(gained_done, 1)

            def ln_offset(n, layer):
                pool.wait_ge(gained_done, G * (n + 1))
                nc.gpsimd.tensor_tensor((h2 if layer else h1)[:], z[:],
                                        offset[:, layer:layer + 1, :].to_broadcast([P, G, H]), ALU.add)\
                  .then_inc(h_done, 1)

            def out_rstd(g):
                pool.wait_ge(out_moments_done, g + 1)
                nc.gpsimd.tensor_tensor(out_var[:], out_moments[:, :, 1], out_eps[:], ALU.add)\
                  .then_inc(out_var_done, 1)
                pool.wait_ge(out_var_done, g + 1)
                nc.gpsimd.tensor_tensor(out_scale[:], out_var[:], minus_half[:], ALU.pow)\
                  .then_inc(out_scale_done, 1)

            def slot(s):
                prev = s.prev_layer is not None

                def hlin_low(b):
                    pool.wait_ge(hlin_hi_done, G * s.n + b + 1)
                    nc.gpsimd.tensor_tensor(hlin_lo[:, b, :], hlin[:, b, :], hlin_hi[:, b, :].bitcast(F32),
                                            ALU.subtract).then_inc(hlin_lo_done, 1)

                def x_low():
                    buf = 1 - s.parity
                    pool.wait_ge(x_hi_done, s.split_group)
                    nc.gpsimd.tensor_tensor(ht_lo[buf][:], x_in[:], ht_hi[buf][:].bitcast(F32),
                                            ALU.subtract).then_inc(x_lo_done, 1)

                if s.late is not None:
                    ln_sigma(s.n - 1)
                    ln_gain(s.n - 1, s.prev_layer)
                    ln_offset(s.n - 1, s.prev_layer)
                    if s.split_group is not None:
                        x_low()
                    for b in range(G):
                        hlin_low(b)
                    return
                if s.split_group is not None:
                    x_low()
                if s.mask_group is not None:
                    mask(s.mask_group, s.mask_buf)
                if s.hurried:
                    ln_sigma(s.n - 1)
                    ln_gain(s.n - 1, s.prev_layer)
                    ln_offset(s.n - 1, s.prev_layer)
                    if s.final is not None:
                        out_rstd(s.final)
                    for b in range(G):
                        hlin_low(b)
                    return
                if s.final is not None:
                    out_rstd(s.final)
                hlin_low(0)
                if prev:
                    ln_sigma(s.n - 1)
                hlin_low(1)
                hlin_low(2)
                hlin_low(3)
                if prev:
                    ln_gain(s.n - 1, s.prev_layer)
                    ln_offset(s.n - 1, s.prev_layer)

            for constant, value in ((half, 0.5), (minus_half, -0.5), (unbiased, H / (H - 1.0)),
                                    (out_eps, OUT_EPS)):
                nc.gpsimd.memset(constant[:], value).then_inc(scalars_set, 1)
            pool.wait_ge(consts_in, 5 * DMA)
            mask(0, 0)
            pool.wait_ge(scalars_set, 4)
            head = head_slots()
            slot(head[0])
            for kind in range(3):
                pool.wait_ge(w_hi1_done, kind + 1)
                nc.gpsimd.tensor_tensor(w_lo[:, 1, kind], raw_w[1][kind], w_hi[:, 1, kind].bitcast(F32),
                                        ALU.subtract).then_inc(w_lo1_done, 1)
            for s in head[1:]:
                slot(s)
            with pool.Fori(0, LOOPS) as r:
                for s in loop_slots(r):
                    slot(s)
            for s in tail_slots():
                slot(s)
            out_rstd(NG - 2)
            ln_sigma(UNITS - 1)
            out_rstd(NG - 1)


def kernel(x, adj, L0_gnn_W_left, L0_gnn_W_right, L0_gnn_W_lin, L0_gnn_b_lin, L0_gnn_ln_a, L0_gnn_ln_b):
    import numpy as np
    import concourse.bacc as bacc
    from concourse.bass_utils import run_bass_kernel_spmd

    x, adj = np.asarray(x), np.asarray(adj)
    x_tok = x.reshape(NG, G, S, H).transpose(0, 2, 1, 3)
    x_feat = x.reshape(NG, G, S, HC, P).transpose(0, 4, 3, 1, 2).reshape(NG, P, HC, TOK)
    adj_tok = adj.reshape(NG, G, S, S).transpose(0, 2, 1, 3)
    adj_t = adj.reshape(NG, G, S, S).transpose(0, 3, 1, 2)
    w = np.stack([np.asarray(a) for a in (L0_gnn_W_left, L0_gnn_W_right, L0_gnn_W_lin)], axis=1)
    w_feat = w.reshape(L, 3, H, HC, P).transpose(0, 1, 4, 3, 2)
    arrays = {
        "x_tok": x_tok, "x_feat": x_feat, "adj_pair": np.stack([adj_tok, adj_t], axis=2),
        "w_feat": w_feat, "b_lin": L0_gnn_b_lin, "ln_a": L0_gnn_ln_a, "ln_b": L0_gnn_ln_b,
        "identity_in": np.eye(S, dtype=np.float32),
        "triangles_in": np.stack([np.triu(np.ones((S, S), np.float32)),
                                  np.tril(np.ones((S, S), np.float32), -1)], axis=1),
    }
    nc = bacc.Bacc("TRN2", target_bir_lowering=False, num_devices=1)
    in_map, args = {}, []
    for name, a in arrays.items():
        a = np.ascontiguousarray(a)
        in_map[name + "_dram"] = a
        args.append(nc.dram_tensor(name + "_dram", a.shape, F32, kind="ExternalInput").ap())
    out = nc.dram_tensor("out_dram", (NG, S, G, H), F32, kind="ExternalOutput").ap()
    build(nc, *args, out)
    r = run_bass_kernel_spmd(nc, [in_map], core_ids=[0])
    got = r.results[0]["out_dram"]
    return np.ascontiguousarray(got.transpose(0, 2, 1, 3).reshape(B, S, H))
```

```python
from contextlib import ExitStack

import concourse.bass as bass
from concourse import mybir

F32 = mybir.dt.float32
F32R = mybir.dt.float32r
ALU = mybir.AluOpType
ACT = mybir.ActivationFunctionType

B, S, H, L = 64, 128, 384, 2
P = 128
G = 512 // S
NG = B // G
HC = H // P
TOK = G * S
TEMPER = float(H) ** 0.5
LN_EPS = 1e-3
SUM_EPS = 1e-10
OUT_EPS = 1e-5
M_TILES = 2 * HC
UNIT_TILES = M_TILES + G
LEFT, RIGHT, LIN = range(3)
ONES = 2
WARM_UP = 9
C_BANKS = 3
DMA = 16


class Slot:

    def __init__(self, n, tile0, layer, prev_layer=None, prev_group=None, prev_mask=None, transposes=None,
                 late_transposes=None, mask_group=None, mask_buf=None, split_group=None,
                 final=None, final_buf=None, parity=0, hurried=False, early=False,
                 group=None, mask=None):
        self.n = n
        self.at = n if isinstance(n, int) else None
        self.tile0 = tile0
        self.layer = layer
        self.prev_layer = prev_layer
        self.prev_group = prev_group
        self.prev_mask = prev_mask
        self.transposes = transposes
        self.late = late_transposes
        self.mask_group = mask_group
        self.mask_buf = mask_buf
        self.split_group = split_group
        self.final = final
        self.final_buf = final_buf
        self.parity = parity
        self.hurried = hurried
        self.early = early
        self.group = group
        self.mask = mask


PAIR_TILES = 2 * UNIT_TILES + HC
PAIRS = NG - 1
UNITS = NG * L


def odd_slot(k, k_parity, first=False):
    return Slot(2 * k + 1, PAIR_TILES * k + UNIT_TILES, 0,
                prev_layer=0 if first else 1, prev_group=0 if first else k - 1,
                prev_mask=0 if first else 1 - k_parity,
                transposes=None if first else k,
                mask_group=k + 1, mask_buf=1 - k_parity, parity=1,
                hurried=first, early=first, group=k + 1, mask=1 - k_parity)


def even_slot(k, k_parity, first=False, last=False):
    return Slot(2 * k + 2, PAIR_TILES * k + 2 * UNIT_TILES + HC, 1,
                prev_layer=0, prev_group=k + 1, prev_mask=1 - k_parity, late_transposes=0 if first else None,
                split_group=None if last else k + 2,
                final=None if first else k - 1, final_buf=None if first else 1 - k_parity,
                parity=0, hurried=last, early=last, group=k, mask=k_parity)


LOOPS = (PAIRS - 3) // 2
assert PAIRS == 3 + 2 * LOOPS


def head_slots():
    return [Slot(0, 0, 0, split_group=1, parity=0),
            odd_slot(0, 0, first=True), even_slot(0, 0, first=True),
            odd_slot(1, 1), even_slot(1, 1)]


def loop_slots(r):
    return [odd_slot(2 * r + 2, 0), even_slot(2 * r + 2, 0),
            odd_slot(2 * r + 3, 1), even_slot(2 * r + 3, 1)]


def tail_slots():
    k = PAIRS - 1
    return [odd_slot(k, k % 2), even_slot(k, k % 2, last=True),
            Slot(UNITS - 1, PAIR_TILES * PAIRS + UNIT_TILES + HC, 1, prev_layer=1,
                 prev_group=NG - 2, prev_mask=(NG - 2) % 2, late_transposes=PAIRS, parity=(UNITS - 1) % 2,
                 early=True, group=NG - 1, mask=(NG - 1) % 2,
                 final=NG - 2, final_buf=(NG - 2) % 2)]


def drained_before(slot, t):
    return slot.tile0 + (t - 2 if t >= 3 else (0, -2, -1)[t])


def build(nc, x_tok, x_feat, adj_pair, w_feat, b_lin, ln_a, ln_b, identity_in, triangles_in, out):
    ctx = ExitStack()
    with ctx:
        def sb(name, shape, dt=F32):
            return ctx.enter_context(nc.sbuf_tensor(name, shape, dt))

        def psum(name, shape):
            return ctx.enter_context(nc.psum_tensor(name, shape, F32))

        def sem(name):
            return ctx.enter_context(nc.semaphore(name))

        identity = sb("identity", [P, S])
        triangles = sb("triangles", [P, 2, S])
        bias = sb("bias", [P, L, H])
        gain = sb("gain", [P, L, H])
        offset = sb("offset", [P, L, H])
        half = sb("half", [P, G])
        minus_half = sb("minus_half", [P, G])
        unbiased = sb("unbiased", [P, G])
        out_eps = sb("out_eps", [P, G])
        w_hi = sb("w_hi", [P, L, 3, HC, H], F32R)
        w_lo = sb("w_lo", [P, L, 3, HC, H], F32R)
        x_in = sb("x_in", [P, HC, TOK])
        adj = [sb(f"adj{i}", [P, 2, G, S]) for i in range(2)]
        gate = [sb(f"gate{i}", [P, 2, G, S]) for i in range(2)]
        residual = [sb(f"residual{i}", [P, G, H]) for i in range(2)]
        ht_hi = [sb(f"ht_hi{i}", [P, HC, TOK], F32R) for i in range(2)]
        ht_lo = [sb(f"ht_lo{i}", [P, HC, TOK], F32R) for i in range(2)]
        m_hi = sb("m_hi", [P, HC, 2, TOK], F32R)
        m_lo = sb("m_lo", [P, HC, 2, TOK], F32R)
        hlin = sb("hlin", [P, G, H])
        hlin_hi = sb("hlin_hi", [P, G, H + ONES], F32R)
        hlin_lo = sb("hlin_lo", [P, G, H + ONES], F32R)
        gated = sb("gated", [P, 2, G, S])
        score = sb("score", [P, G, S])
        expd = sb("expd", [P, G, S])
        delta = sb("delta", [P, G, S])
        att_hi = sb("att_hi", [P, G, S], F32R)
        att_lo = sb("att_lo", [P, G, S], F32R)
        row_den = sb("row_den", [P, G])
        row_scale = sb("row_scale", [P, G])
        z = sb("z", [P, G, H])
        stats = sb("stats", [P, G, 6])
        moments = sb("moments", [P, G, 2])
        variance = sb("variance", [P, G])
        sigma = sb("sigma", [P, G])
        ln_den = sb("ln_den", [P, G])
        ln_scale = sb("ln_scale", [P, G])
        ln_shift = sb("ln_shift", [P, G])
        h1 = sb("h1", [P, G, H])
        h2 = sb("h2", [P, G, H])
        out_stats = sb("out_stats", [P, G, 6])
        out_moments = sb("out_moments", [P, G, 2])
        out_var = sb("out_var", [P, G])
        out_scale = sb("out_scale", [P, G])
        out_shift = sb("out_shift", [P, G])
        result = sb("result", [P, G, H])
        raw_w = [[b[:].rearrange("p b h -> p (b h)")[:, 0:HC * H].rearrange("p (c o) -> p c o", c=HC)
                  for b in bufs] for bufs in ((z, h1, h2), (residual[0], residual[1], result))]

        tile = [psum(f"tile{i}", [P, TOK]) for i in range(3)]
        u_bank = [psum(f"u_bank{i}", [P, 2, 2, S]) for i in range(2)]
        c_bank = [psum(f"c_bank{i}", [P, H + ONES]) for i in range(C_BANKS)]

        w_in = [[sem(f"w_in{l}{k}") for k in range(3)] for l in range(L)]
        consts_in = sem("consts_in")
        x0_landed = [sem(f"x0_landed{c}") for c in range(HC)]
        x_landed = sem("x_landed")
        wl_landed = [sem(f"wl_landed{c}") for c in range(HC)]
        adj_landed = sem("adj_landed")
        residual_landed = [sem(f"residual_landed{i}") for i in range(2)]
        stored = sem("stored")
        tile_full = sem("tile_full")
        u_full = sem("u_full")
        c_full = sem("c_full")
        w_hi0_done = sem("w_hi0_done")
        w_hi1_done = sem("w_hi1_done")
        m_hi_done = sem("m_hi_done")
        hlin_hi_done = sem("hlin_hi_done")
        ht_hi_done = sem("ht_hi_done")
        exp_done = sem("exp_done")
        att_hi_done = sem("att_hi_done")
        z_done = sem("z_done")
        norm_done = sem("norm_done")
        tile_drained = sem("tile_drained")
        w_lo0_done = sem("w_lo0_done")
        x_hi0_done = sem("x_hi0_done")
        x_hi_done = sem("x_hi_done")
        gated_done = sem("gated_done")
        score_done = sem("score_done")
        delta_done = sem("delta_done")
        row_den_done = sem("row_den_done")
        row_scale_done = sem("row_scale_done")
        att_lo_done = sem("att_lo_done")
        stats_done = sem("stats_done")
        moments_done = sem("moments_done")
        ln_den_done = sem("ln_den_done")
        ln_scale_done = sem("ln_scale_done")
        ln_shift_done = sem("ln_shift_done")
        summed_done = sem("summed_done")
        out_stats_done = sem("out_stats_done")
        out_moments_done = sem("out_moments_done")
        result_done = sem("result_done")
        last_h_done = sem("last_h_done")
        x_lo0_done = sem("x_lo0_done")
        warm_zeros_set = sem("warm_zeros_set")
        scalars_set = sem("scalars_set")
        ones_set = sem("ones_set")
        w_lo1_done = sem("w_lo1_done")
        x_lo_done = sem("x_lo_done")
        gate_done = sem("gate_done")
        hlin_lo_done = sem("hlin_lo_done")
        variance_done = sem("variance_done")
        sigma_done = sem("sigma_done")
        gained_done = sem("gained_done")
        h_done = sem("h_done")
        out_var_done = sem("out_var_done")
        out_scale_done = sem("out_scale_done")
        out_shift_done = sem("out_shift_done")

        block = ctx.enter_context(nc.Block())

        def chunk(b):
            return slice(b * S, (b + 1) * S)

        def batches(halves):
            return slice(2 * halves[0], 2 * halves[-1] + 2)

        @block.sync
        def _(sp):
            for c in range(HC):
                sp.dma_start(x_in[:, c], x_feat[0, :, c]).then_inc(x0_landed[c], DMA)
                sp.dma_start(raw_w[0][LEFT][:, c], w_feat[0, LEFT, :, c]).then_inc(wl_landed[c], DMA)
            sp.dma_start(raw_w[0][RIGHT], w_feat[0, RIGHT]).then_inc(w_in[0][RIGHT], DMA)
            sp.dma_start(raw_w[0][LIN], w_feat[0, LIN]).then_inc(w_in[0][LIN], DMA)
            sp.dma_start(bias[:], b_lin.partition_broadcast(P)).then_inc(consts_in, DMA)
            sp.dma_start(identity[:], identity_in).then_inc(consts_in, DMA)
            sp.dma_start(triangles[:], triangles_in).then_inc(consts_in, DMA)
            sp.dma_start(gain[:], ln_a.partition_broadcast(P)).then_inc(consts_in, DMA)
            sp.dma_start(offset[:], ln_b.partition_broadcast(P)).then_inc(consts_in, DMA)
            sp.dma_start(adj[0][:], adj_pair[0]).then_inc(adj_landed, DMA)
            sp.wait_ge(x_lo0_done, HC)
            sp.dma_start(x_in[:], x_feat[1]).then_inc(x_landed, DMA)
            for kind in range(3):
                sp.dma_start(raw_w[1][kind], w_feat[1, kind]).then_inc(w_in[1][kind], DMA)
            sp.wait_ge(adj_landed, DMA)
            sp.dma_start(adj[1][:], adj_pair[1]).then_inc(adj_landed, DMA)

            def load_x(k):
                sp.wait_ge(x_lo_done, k + 1)
                sp.dma_start(x_in[:], x_feat[k + 2]).then_inc(x_landed, DMA)

            def load_adj(k, k_parity):
                sp.wait_ge(delta_done, 2 * (2 * k + 1))
                sp.dma_start(adj[1 - k_parity][:], adj_pair[k + 1]).then_inc(adj_landed, DMA)

            def load_residual(g, g_parity):
                sp.dma_start(residual[g_parity][:], x_tok[g]).then_inc(residual_landed[g_parity], DMA)

            def store(g):
                sp.wait_ge(result_done, G * (g + 1))
                sp.dma_start(out[g], result[:]).then_inc(stored, DMA)

            def pair(k, k_parity):
                load_x(k)
                load_adj(k, k_parity)
                load_residual(k, k_parity)
                store(k - 1)

            load_x(0)
            sp.wait_ge(w_lo1_done, 3)
            load_residual(0, 0)
            pair(1, 1)
            with sp.Fori(0, LOOPS) as r:
                pair(2 * r + 2, 0)
                pair(2 * r + 3, 1)
            k = PAIRS - 1
            load_adj(k, k % 2)
            load_residual(k, k % 2)
            store(k - 1)
            load_residual(NG - 1, (NG - 1) % 2)
            store(NG - 2)
            for b in range(G):
                sp.wait_ge(result_done, G * (NG - 1) + b + 1)
                sp.dma_start(out[NG - 1, :, b], result[:, b]).then_inc(stored, DMA)
            sp.wait_ge(stored, DMA * (NG - 1 + G))

        @block.tensor
        def _(pe):
            def passes(dst, lhs_hi, lhs_lo, rhs_hi, rhs_lo, first, last):
                nc.tensor.matmul(dst, lhs_hi, rhs_hi, start=first, stop=False)
                nc.tensor.matmul(dst, lhs_hi, rhs_lo, start=False, stop=False)
                return nc.tensor.matmul(dst, lhs_lo, rhs_hi, start=False, stop=last)

            def context(n, b):
                if b % 2 == 0:
                    pe.wait_ge(att_lo_done, 2 * n + b // 2 + 1)
                if b == 0:
                    if isinstance(n, int) and n == 0:
                        pe.wait_ge(ones_set, 2)
                    else:
                        pe.wait_ge(z_done, G * n)
                elif b == C_BANKS:
                    pe.wait_ge(z_done, G * n + 1)
                pe.wait_ge(hlin_lo_done, G * n + b + 1)
                passes(c_bank[b % C_BANKS][:], att_hi[:, b], att_lo[:, b],
                       hlin_hi[:, b, :], hlin_lo[:, b, :], True, True).then_inc(c_full, 1)

            def slot(s):
                hi, lo = ht_hi[s.parity], ht_lo[s.parity]
                prev = s.prev_layer is not None

                def project(t):
                    side, oc = t // HC, t % HC
                    pe.wait_ge(tile_drained, drained_before(s, t))
                    if s.at == 0 and t == HC:
                        pe.wait_ge(w_lo0_done, HC + 1)
                    for hc in range(HC):
                        last = passes(tile[t % 3][:],
                                      w_hi[:, s.layer, side, hc, chunk(oc)],
                                      w_lo[:, s.layer, side, hc, chunk(oc)],
                                      hi[:, hc, :], lo[:, hc, :], hc == 0, hc == HC - 1)
                    last.then_inc(tile_full, 1)

                def project_first():
                    for hc in range(HC):
                        pe.wait_ge(x_lo0_done, hc + 1)
                        pe.wait_ge(w_lo0_done, hc + 1)
                        for t in range(HC):
                            last = passes(tile[t][:], w_hi[:, 0, LEFT, hc, chunk(t)],
                                          w_lo[:, 0, LEFT, hc, chunk(t)],
                                          hi[:, hc, :], lo[:, hc, :], hc == 0, hc == HC - 1)
                            if hc == HC - 1:
                                last.then_inc(tile_full, 1)

                def linear(b):
                    t = M_TILES + b
                    pe.wait_ge(tile_drained, drained_before(s, t))
                    if s.at == 0 and b == 0:
                        pe.wait_ge(w_lo0_done, HC + 2)
                    for hc in range(HC):
                        last = passes(tile[t % 3][:, 0:H], hi[:, hc, chunk(b)], lo[:, hc, chunk(b)],
                                      w_hi[:, s.layer, LIN, hc, :], w_lo[:, s.layer, LIN, hc, :],
                                      hc == 0, hc == HC - 1)
                    last.then_inc(tile_full, 1)

                def transpose_h(hc, tile0, h_count):
                    if hc == 0:
                        pe.wait_ge(h_done, h_count)
                        if s.at == 2:
                            pe.wait_ge(consts_in, 5 * DMA)
                    t = UNIT_TILES + hc
                    pe.wait_ge(tile_drained, tile0 + t - 2)
                    for b in range(G):
                        last = nc.tensor.transpose(tile[t % 3][:, chunk(b)], h1[:, b, chunk(hc)],
                                                   identity[:])
                    last.then_inc(tile_full, 1)

                def scores(b):
                    if b == 0:
                        pe.wait_ge(tile_drained, s.tile0 + M_TILES)
                    if b % 2 == 0 and s.at != 0:
                        pe.wait_ge(gated_done, 2 * (s.n - 1) + b // 2 + 1)
                    for hc in range(HC):
                        last = passes(u_bank[b // 2][:, b % 2, :, :], hi[:, hc, chunk(b)], lo[:, hc, chunk(b)],
                                      m_hi[:, hc, :, chunk(b)], m_lo[:, hc, :, chunk(b)],
                                      hc == 0, hc == HC - 1)
                    if b % 2 == 1:
                        last.then_inc(u_full, 1)

                if s.late is not None:
                    for hc in range(HC):
                        transpose_h(hc, s.tile0 - HC - UNIT_TILES, s.n - 1)
                    context(s.n - 1, 0)
                    context(s.n - 1, 1)
                    context(s.n - 1, 2)
                    pe.wait_ge(tile_drained, s.tile0)
                    if s.n == 2:
                        pe.wait_ge(w_lo1_done, 3)
                    project(0)
                    context(s.n - 1, 3)
                    for t in range(1, M_TILES):
                        project(t)
                    for b in range(2 if s.early else G):
                        linear(b)
                elif s.hurried:
                    if s.layer == 0:
                        pe.wait_ge(x_lo_done, s.mask_group)
                    for t in range(HC):
                        project(t)
                    context(s.n - 1, 0)
                    context(s.n - 1, 1)
                    project(3)
                    context(s.n - 1, 2)
                    context(s.n - 1, 3)
                    project(4)
                    project(5)
                    linear(0)
                    linear(1)
                else:
                    if s.layer == 0 and s.at != 0:
                        pe.wait_ge(x_lo_done, s.mask_group)
                    if s.at == 0:
                        project_first()
                    for t in range(HC if s.at == 0 else 0, M_TILES):
                        project(t)
                    if prev:
                        context(s.n - 1, 0)
                        context(s.n - 1, 1)
                    linear(0)
                    if prev:
                        context(s.n - 1, 2)
                        context(s.n - 1, 3)
                    for b in range(1, G):
                        linear(b)
                if s.transposes is not None:
                    transpose_h(0, s.tile0, s.n - 1)
                    transpose_h(1, s.tile0, s.n - 1)
                scores(0)
                if s.transposes is not None:
                    transpose_h(2, s.tile0, s.n - 1)
                for b in range(1, G):
                    scores(b)
                if s.early:
                    linear(2)
                    linear(3)

            pe.wait_ge(warm_zeros_set, 1)
            for _ in range(WARM_UP):
                nc.tensor.matmul(u_bank[0][:], m_lo[:, 0, 0, 0:P], m_lo[:, 0, 0, :], start=True, stop=True)
            for s in head_slots():
                slot(s)
            with pe.Fori(0, LOOPS) as r:
                for s in loop_slots(r):
                    slot(s)
            for s in tail_slots():
                slot(s)
            for b in range(G):
                context(UNITS - 1, b)

        @block.scalar
        def _(act):
            def exponent(n, halves=(0, 1)):
                act.wait_ge(score_done, 2 * n + halves[-1] + 1)
                nc.scalar.activation(expd[:, batches(halves)], score[:, batches(halves)], ACT.Exp,
                                     scale=1.0 / TEMPER).then_inc(exp_done, len(halves))

            def attention_high(n, halves=(0, 1)):
                act.wait_ge(delta_done, 2 * n + halves[-1] + 1)
                nc.scalar.activation(att_hi[:, batches(halves)], delta[:, batches(halves)], ACT.Copy)\
                  .then_inc(att_hi_done, len(halves))

            def context_out(n, b):
                if b % 2 == 0:
                    act.wait_ge(row_scale_done, 2 * n + b // 2 + 1)
                if b == 0:
                    if isinstance(n, int) and n == UNITS - 1:
                        act.wait_ge(last_h_done, G)
                    elif not isinstance(n, int) or n > 0:
                        act.wait_ge(h_done, n)
                nc.scalar.activation(z[:, b, :], c_bank[b % C_BANKS][:, 0:H], ACT.Copy,
                                     scale=row_scale[:, b:b + 1]).then_inc(z_done, 1)

            def normalise(n):
                act.wait_ge(ln_shift_done, n + 1)
                for b in range(G):
                    nc.scalar.activation(z[:, b, :], z[:, b, :], ACT.Identity, bias=ln_shift[:, b:b + 1],
                                         scale=ln_scale[:, b:b + 1]).then_inc(norm_done, 1)

            def first_weights_high(kind):
                act.wait_ge(w_in[0][kind], DMA)
                nc.scalar.activation(w_hi[:, 0, kind], raw_w[0][kind], ACT.Copy).then_inc(w_hi0_done, 1)

            def slot(s):
                prev = s.prev_layer is not None

                def m_high(t):
                    act.wait_ge(tile_full, s.tile0 + t + 1)
                    nc.scalar.activation(m_hi[:, t % HC, t // HC, :], tile[t % 3][:], ACT.Copy)\
                      .then_inc(m_hi_done, 1)

                def hlin_high(b):
                    act.wait_ge(tile_drained, s.tile0 + M_TILES + b + 1)
                    nc.scalar.activation(hlin_hi[:, b, 0:H], hlin[:, b, :], ACT.Copy)\
                      .then_inc(hlin_hi_done, 1)

                def h_high(hc, tile0, buf):
                    act.wait_ge(tile_full, tile0 + UNIT_TILES + hc + 1)
                    nc.scalar.activation(ht_hi[buf][:, hc, :], tile[(UNIT_TILES + hc) % 3][:], ACT.Relu)\
                      .then_inc(ht_hi_done, 1)

                if prev and s.late is None:
                    exponent(s.n - 1)
                if s.late is not None:
                    for hc in range(HC):
                        h_high(hc, s.tile0 - HC - UNIT_TILES, s.parity)
                    context_out(s.n - 1, 0)
                    context_out(s.n - 1, 1)
                    m_high(0)
                    context_out(s.n - 1, 2)
                    context_out(s.n - 1, 3)
                    for t in range(1, 4):
                        m_high(t)
                    if s.final is None:
                        normalise(s.n - 1)
                    for t in range(4, M_TILES):
                        m_high(t)
                    hlin_high(0)
                    hlin_high(1)
                elif s.hurried:
                    m_high(0)
                    attention_high(s.n - 1)
                    m_high(1)
                    m_high(2)
                    context_out(s.n - 1, 0)
                    context_out(s.n - 1, 1)
                    m_high(3)
                    context_out(s.n - 1, 2)
                    context_out(s.n - 1, 3)
                    m_high(4)
                    m_high(5)
                    normalise(s.n - 1)
                    hlin_high(0)
                    hlin_high(1)
                else:
                    m_high(0)
                    if prev:
                        attention_high(s.n - 1)
                    m_high(1)
                    m_high(2)
                    if s.at == 0:
                        first_weights_high(LIN)
                    for t in range(3, M_TILES):
                        m_high(t)
                    if prev:
                        context_out(s.n - 1, 0)
                        context_out(s.n - 1, 1)
                    hlin_high(0)
                    if prev:
                        context_out(s.n - 1, 2)
                        context_out(s.n - 1, 3)
                    hlin_high(1)
                    hlin_high(2)
                    if s.transposes is not None:
                        h_high(0, s.tile0, 1 - s.parity)
                        h_high(1, s.tile0, 1 - s.parity)
                    hlin_high(3)
                    if s.transposes is not None:
                        h_high(2, s.tile0, 1 - s.parity)
                    if prev:
                        normalise(s.n - 1)
                if s.early:
                    exponent(s.n, (0,))
                    attention_high(s.n, (0,))
                    exponent(s.n, (1,))
                    hlin_high(2)
                    attention_high(s.n, (1,))
                    hlin_high(3)
                elif s.late is not None:
                    hlin_high(2)
                    hlin_high(3)

            for c in range(HC):
                act.wait_ge(wl_landed[c], DMA)
                nc.scalar.activation(w_hi[:, 0, LEFT, c], raw_w[0][LEFT][:, c], ACT.Copy)\
                  .then_inc(w_hi0_done, 1)
            first_weights_high(RIGHT)
            head = head_slots()
            slot(head[0])
            for kind in range(3):
                act.wait_ge(w_in[1][kind], DMA)
                nc.scalar.activation(w_hi[:, 1, kind], raw_w[1][kind], ACT.Copy).then_inc(w_hi1_done, 1)
            for s in head[1:]:
                slot(s)
            with act.Fori(0, LOOPS) as r:
                for s in loop_slots(r):
                    slot(s)
            for s in tail_slots():
                slot(s)
            for b in range(G):
                context_out(UNITS - 1, b)
            g, buf = NG - 2, (NG - 2) % 2
            act.wait_ge(out_shift_done, 1)
            act.wait_ge(stored, DMA * g)
            for b in range(G):
                nc.scalar.activation(result[:, b], residual[buf][:, b], ACT.Identity,
                                     bias=out_shift[:, b:b + 1], scale=out_scale[:, b:b + 1])\
                  .then_inc(result_done, 1)

        @block.vector
        def _(dve):
            def gate_scores(n, group, buf, halves=(0, 1)):
                dve.wait_ge(gate_done, group + 1)
                for k in halves:
                    dve.wait_ge(u_full, 2 * n + k + 1)
                    nc.vector.tensor_tensor(
                        gated[:, :, 2 * k:2 * k + 2, :], u_bank[k][:].rearrange("p b s j -> p s b j"),
                        gate[buf][:, :, 2 * k:2 * k + 2, :], ALU.mult).then_inc(gated_done, 1)

            def add_sides(n, halves=(0, 1)):
                dve.wait_ge(gated_done, 2 * n + halves[-1] + 1)
                nc.vector.tensor_tensor(score[:, batches(halves)], gated[:, 0, batches(halves)],
                                        gated[:, 1, batches(halves)], ALU.add)\
                  .then_inc(score_done, len(halves))

            def attend(n, buf, halves=(0, 1)):
                dve.wait_ge(exp_done, 2 * n + halves[-1] + 1)
                nc.vector.tensor_tensor(delta[:, batches(halves)], expd[:, batches(halves)],
                                        adj[buf][:, 0, batches(halves)], ALU.mult)\
                  .then_inc(delta_done, len(halves))

            def row_scales(n, k):
                for b in (2 * k, 2 * k + 1):
                    dve.wait_ge(c_full, G * n + b + 1)
                    nc.vector.tensor_scalar(row_den[:, b:b + 1], c_bank[b % C_BANKS][:, H:H + 1],
                                            SUM_EPS, None, ALU.add).then_inc(row_den_done, 1)
                dve.wait_ge(row_den_done, G * n + 2 * k + 2)
                nc.vector.reciprocal(row_scale[:, 2 * k:2 * k + 2], row_den[:, 2 * k:2 * k + 2])\
                  .then_inc(row_scale_done, 1)

            def attention_low(n, halves=(0, 1)):
                dve.wait_ge(att_hi_done, 2 * n + halves[-1] + 1)
                nc.vector.tensor_tensor(att_lo[:, batches(halves)], delta[:, batches(halves)],
                                        att_hi[:, batches(halves)].bitcast(F32), ALU.subtract)\
                  .then_inc(att_lo_done, len(halves))

            def ln_stats(n, which):
                for b in which:
                    dve.wait_ge(z_done, G * n + b + 1)
                    nc.vector.bn_stats(stats[:, b, :], z[:, b, :]).then_inc(stats_done, 1)

            def ln_moments():
                for b in range(G):
                    last = nc.vector.bn_aggr(moments[:, b, :], stats[:, b, :])
                last.then_inc(moments_done, 1)

            def ln_scales(n):
                dve.wait_ge(sigma_done, n + 1)
                nc.vector.tensor_scalar(ln_den[:], sigma[:], LN_EPS, None, ALU.add)\
                  .then_inc(ln_den_done, 1)
                dve.wait_ge(ln_den_done, n + 1)
                nc.vector.reciprocal(ln_scale[:], ln_den[:]).then_inc(ln_scale_done, 1)
                dve.wait_ge(ln_scale_done, n + 1)
                nc.vector.scalar_tensor_tensor(out=ln_shift[:], in0=moments[:, :, 0], scalar=-1.0,
                                               in1=ln_scale[:], op0=ALU.mult, op1=ALU.mult)\
                  .then_inc(ln_shift_done, 1)

            def out_sum(g, buf, b):
                nc.vector.scalar_tensor_tensor(out=residual[buf][:, b], in0=h2[:, b], scalar=0.0,
                                               in1=residual[buf][:, b], op0=ALU.max, op1=ALU.add)\
                  .then_inc(summed_done, 1)

            def residual_ready(g, buf):
                dve.wait_ge(residual_landed[buf], DMA // 2 * (g - buf) + DMA)

            def out_statistics(g, buf, which):
                for b in which:
                    dve.wait_ge(summed_done, G * g + b + 1)
                    nc.vector.bn_stats(out_stats[:, b, :], residual[buf][:, b, :])\
                      .then_inc(out_stats_done, 1)

            def out_aggregate(which=range(G)):
                for b in which:
                    last = nc.vector.bn_aggr(out_moments[:, b, :], out_stats[:, b, :])
                last.then_inc(out_moments_done, 1)

            def out_normalise(g, buf, which=range(G)):
                for b in which:
                    nc.vector.tensor_scalar(result[:, b, :], residual[buf][:, b, :],
                                            out_moments[:, b, 0:1], out_scale[:, b:b + 1],
                                            ALU.subtract, ALU.mult).then_inc(result_done, 1)

            def centre(n, which):
                for b in which:
                    nc.vector.scalar_tensor_tensor(out=z[:, b], in0=z[:, b], scalar=moments[:, b, 0:1],
                                                   in1=gain[:, 1], op0=ALU.subtract, op1=ALU.mult)\
                      .then_inc(gained_done, 1)

            def last_h(n, b):
                dve.wait_ge(gained_done, G * n + b + 1)
                nc.vector.scalar_tensor_tensor(out=h2[:, b], in0=z[:, b], scalar=ln_scale[:, b:b + 1],
                                               in1=offset[:, 1], op0=ALU.mult, op1=ALU.add)\
                  .then_inc(last_h_done, 1)

            def slot(s):
                prev, final = s.prev_layer is not None, s.final is not None

                def m_low(t):
                    dve.wait_ge(m_hi_done, M_TILES * s.n + t + 1)
                    nc.vector.tensor_tensor(m_lo[:, t % HC, t // HC, :], tile[t % 3][:],
                                            m_hi[:, t % HC, t // HC, :].bitcast(F32), ALU.subtract)\
                      .then_inc(tile_drained, 1)

                def x_high():
                    dve.wait_ge(x_landed, DMA * s.split_group)
                    nc.vector.tensor_copy(ht_hi[1 - s.parity][:], x_in[:]).then_inc(x_hi_done, 1)

                def h_low(hc, buf, second):
                    dve.wait_ge(ht_hi_done, HC * second + hc + 1)
                    nc.vector.scalar_tensor_tensor(
                        out=ht_lo[buf][:, hc, :], in0=tile[(UNIT_TILES + hc) % 3][:], scalar=0.0,
                        in1=ht_hi[buf][:, hc, :].bitcast(F32), op0=ALU.max, op1=ALU.subtract)\
                      .then_inc(tile_drained, 1)

                def hlin_bias(b):
                    dve.wait_ge(tile_full, s.tile0 + M_TILES + b + 1)
                    if s.at == 0 and b == 0:
                        dve.wait_ge(consts_in, 5 * DMA)
                    elif s.at != 0:
                        dve.wait_ge(hlin_lo_done, G * (s.n - 1) + b + 1)
                    nc.vector.tensor_tensor(hlin[:, b, :], tile[(M_TILES + b) % 3][:, 0:H],
                                            bias[:, s.layer, :], ALU.add).then_inc(tile_drained, 1)

                def final_sum():
                    dve.wait_ge(h_done, s.n - 1)
                    residual_ready(s.final, s.final_buf)
                    for b in range(G):
                        out_sum(s.final, s.final_buf, b)

                def final_normalise():
                    dve.wait_ge(out_scale_done, s.final + 1)
                    if not isinstance(s.final, int) or s.final > 0:
                        dve.wait_ge(stored, DMA * s.final)
                    out_normalise(s.final, s.final_buf)

                def w_low(kind):
                    dve.wait_ge(w_hi0_done, HC + kind)
                    nc.vector.tensor_tensor(w_lo[:, 0, kind], raw_w[0][kind], w_hi[:, 0, kind].bitcast(F32),
                                            ALU.subtract).then_inc(w_lo0_done, 1)

                def early_softmax():
                    gate_scores(s.n, s.group, s.mask, (0,))
                    add_sides(s.n, (0,))
                    if s.late is not None:
                        out_statistics(s.final, s.final_buf, (2,))
                    attend(s.n, s.mask, (0,))
                    gate_scores(s.n, s.group, s.mask, (1,))
                    attention_low(s.n, (0,))
                    add_sides(s.n, (1,))
                    hlin_bias(2)
                    attend(s.n, s.mask, (1,))
                    hlin_bias(3)
                    attention_low(s.n, (1,))

                if prev and s.late is None:
                    gate_scores(s.n - 1, s.prev_group, s.prev_mask)
                    add_sides(s.n - 1)
                    attend(s.n - 1, s.prev_mask)
                if s.hurried:
                    m_low(0)
                    attention_low(s.n - 1)
                    m_low(1)
                    if final:
                        final_sum()
                    m_low(2)
                    row_scales(s.n - 1, 0)
                    ln_stats(s.n - 1, (0, 1))
                    m_low(3)
                    row_scales(s.n - 1, 1)
                    if final:
                        out_statistics(s.final, s.final_buf, (0, 1))
                    ln_stats(s.n - 1, (2, 3))
                    dve.wait_ge(stats_done, G * s.n)
                    ln_moments()
                    if final:
                        out_statistics(s.final, s.final_buf, (2, 3))
                    m_low(4)
                    if final:
                        dve.wait_ge(out_stats_done, G * (s.final + 1))
                        out_aggregate()
                    ln_scales(s.n - 1)
                    m_low(5)
                    hlin_bias(0)
                    hlin_bias(1)
                    if final:
                        final_normalise()
                    early_softmax()
                    return
                if s.late is not None:
                    for hc in range(HC):
                        h_low(hc, s.parity, s.late)
                    row_scales(s.n - 1, 0)
                    ln_stats(s.n - 1, (0, 1))
                    m_low(0)
                    row_scales(s.n - 1, 1)
                    ln_stats(s.n - 1, (2, 3))
                    dve.wait_ge(stats_done, G * s.n)
                    m_low(1)
                    ln_moments()
                    if final:
                        dve.wait_ge(moments_done, s.n)
                        centre(s.n - 1, (0, 1))
                        m_low(2)
                        centre(s.n - 1, (2, 3))
                        ln_scales(s.n - 1)
                        dve.wait_ge(summed_done, G * s.final)
                        dve.wait_ge(ln_scale_done, s.n)
                        m_low(3)
                        last_h(s.n - 1, 0)
                        last_h(s.n - 1, 1)
                        m_low(4)
                        last_h(s.n - 1, 2)
                        last_h(s.n - 1, 3)
                        m_low(5)
                        dve.wait_ge(last_h_done, G)
                        residual_ready(s.final, s.final_buf)
                        for b in range(G):
                            out_sum(s.final, s.final_buf, b)
                    else:
                        m_low(2)
                        ln_scales(s.n - 1)
                        for t in range(3, M_TILES):
                            m_low(t)
                    if s.split_group is not None:
                        x_high()
                    hlin_bias(0)
                    if final:
                        out_statistics(s.final, s.final_buf, (0, 1))
                    hlin_bias(1)
                    if s.early:
                        early_softmax()
                    else:
                        hlin_bias(2)
                        hlin_bias(3)
                    return
                if s.at == 0:
                    w_low(RIGHT)
                m_low(0)
                if s.split_group is not None and s.at != 0:
                    x_high()
                m_low(1)
                if final:
                    final_sum()
                m_low(2)
                if s.at == 0:
                    m_low(3)
                    w_low(LIN)
                if prev:
                    attention_low(s.n - 1)
                if final:
                    out_statistics(s.final, s.final_buf, range(G))
                    dve.wait_ge(out_stats_done, G * (s.final + 1))
                if s.at != 0:
                    m_low(3)
                if final:
                    out_aggregate()
                m_low(4)
                m_low(5)
                if s.at == 0:
                    x_high()
                if prev:
                    row_scales(s.n - 1, 0)
                    ln_stats(s.n - 1, (0, 1))
                hlin_bias(0)
                if prev:
                    row_scales(s.n - 1, 1)
                    ln_stats(s.n - 1, (2, 3))
                    dve.wait_ge(stats_done, G * s.n)
                hlin_bias(1)
                if prev:
                    ln_moments()
                hlin_bias(2)
                if prev:
                    ln_scales(s.n - 1)
                hlin_bias(3)
                if final:
                    final_normalise()
                if s.transposes is not None:
                    for hc in range(HC):
                        h_low(hc, 1 - s.parity, s.transposes)

            nc.vector.memset(m_lo[:, 0, 0, :].bitcast(F32), 0.0).then_inc(warm_zeros_set, 1)
            for c in range(HC):
                dve.wait_ge(x0_landed[c], DMA)
                nc.vector.tensor_copy(ht_hi[0][:, c], x_in[:, c]).then_inc(x_hi0_done, 1)
                dve.wait_ge(x_hi0_done, c + 1)
                nc.vector.tensor_tensor(ht_lo[0][:, c], x_in[:, c], ht_hi[0][:, c].bitcast(F32),
                                        ALU.subtract).then_inc(x_lo0_done, 1)
                dve.wait_ge(w_hi0_done, c + 1)
                nc.vector.tensor_tensor(w_lo[:, 0, LEFT, c], raw_w[0][LEFT][:, c],
                                        w_hi[:, 0, LEFT, c].bitcast(F32), ALU.subtract)\
                  .then_inc(w_lo0_done, 1)
            for s in head_slots():
                slot(s)
            with dve.Fori(0, LOOPS) as r:
                for s in loop_slots(r):
                    slot(s)
            for s in tail_slots():
                slot(s)

            n, g = UNITS - 1, NG - 1
            row_scales(n, 0)
            out_statistics(g - 1, (g - 1) % 2, (3,))
            ln_stats(n, (0,))
            dve.wait_ge(out_stats_done, G * g)
            out_aggregate()
            row_scales(n, 1)
            ln_stats(n, (1,))
            dve.wait_ge(out_scale_done, g)
            nc.vector.scalar_tensor_tensor(out=out_shift[:], in0=out_moments[:, :, 0], scalar=-1.0,
                                           in1=out_scale[:], op0=ALU.mult, op1=ALU.mult)\
              .then_inc(out_shift_done, 1)
            ln_stats(n, (2, 3))
            dve.wait_ge(stats_done, G * (n + 1))
            ln_moments()
            dve.wait_ge(moments_done, n + 1)
            centre(n, range(G))
            ln_scales(n)
            residual_ready(g, g % 2)
            dve.wait_ge(summed_done, G * g)
            dve.wait_ge(ln_scale_done, n + 1)
            for step in range(G + 2):
                if step < G:
                    last_h(n, step)
                if 1 <= step <= G:
                    dve.wait_ge(last_h_done, G + step)
                    out_sum(g, g % 2, step - 1)
                if step >= 2:
                    out_statistics(g, g % 2, (step - 2,))
                if step == 3:
                    dve.wait_ge(out_stats_done, G * g + 2)
                    dve.wait_ge(result_done, G * g)
                    out_aggregate((0, 1))
            dve.wait_ge(out_stats_done, G * (g + 1))
            out_aggregate((2, 3))
            dve.wait_ge(stored, DMA * g)
            dve.wait_ge(out_scale_done, g + 1)
            out_normalise(g, g % 2, (0, 1))
            dve.wait_ge(out_scale_done, g + 2)
            out_normalise(g, g % 2, (2, 3))

        @block.gpsimd
        def _(pool):
            def mask(group, buf):
                pool.wait_ge(adj_landed, DMA * (group + 1))
                nc.gpsimd.tensor_tensor(gate[buf][:], adj[buf][:],
                                        triangles[:].unsqueeze(2).to_broadcast([P, 2, G, S]),
                                        ALU.mult).then_inc(gate_done, 1)

            def ln_sigma(n):
                pool.wait_ge(moments_done, n + 1)
                nc.gpsimd.tensor_tensor(variance[:], moments[:, :, 1], unbiased[:], ALU.mult)\
                  .then_inc(variance_done, 1)
                pool.wait_ge(variance_done, n + 1)
                nc.gpsimd.tensor_tensor(sigma[:], variance[:], half[:], ALU.pow).then_inc(sigma_done, 1)

            def ln_gain(n, layer):
                for b in range(G):
                    pool.wait_ge(norm_done, G * n + b + 1)
                    nc.gpsimd.tensor_tensor(z[:, b], z[:, b], gain[:, layer], ALU.mult)\
                      .then_inc(gained_done, 1)

            def ln_offset(n, layer):
                pool.wait_ge(gained_done, G * (n + 1))
                nc.gpsimd.tensor_tensor((h2 if layer else h1)[:], z[:],
                                        offset[:, layer:layer + 1, :].to_broadcast([P, G, H]), ALU.add)\
                  .then_inc(h_done, 1)

            def out_rstd(count, b0=0, b1=G):
                pool.wait_ge(out_moments_done, count)
                nc.gpsimd.tensor_tensor(out_var[:, b0:b1], out_moments[:, b0:b1, 1], out_eps[:, b0:b1],
                                        ALU.add).then_inc(out_var_done, 1)
                pool.wait_ge(out_var_done, count)
                nc.gpsimd.tensor_tensor(out_scale[:, b0:b1], out_var[:, b0:b1], minus_half[:, b0:b1],
                                        ALU.pow).then_inc(out_scale_done, 1)

            def slot(s):
                prev = s.prev_layer is not None

                def hlin_low(b):
                    pool.wait_ge(hlin_hi_done, G * s.n + b + 1)
                    nc.gpsimd.tensor_tensor(hlin_lo[:, b, 0:H], hlin[:, b, :], hlin_hi[:, b, 0:H].bitcast(F32),
                                            ALU.subtract).then_inc(hlin_lo_done, 1)

                def x_low():
                    buf = 1 - s.parity
                    pool.wait_ge(x_hi_done, s.split_group)
                    nc.gpsimd.tensor_tensor(ht_lo[buf][:], x_in[:], ht_hi[buf][:].bitcast(F32),
                                            ALU.subtract).then_inc(x_lo_done, 1)

                if s.late is not None:
                    ln_sigma(s.n - 1)
                    if s.final is None:
                        ln_gain(s.n - 1, s.prev_layer)
                        ln_offset(s.n - 1, s.prev_layer)
                    if s.split_group is not None:
                        x_low()
                    for b in range(G):
                        hlin_low(b)
                    return
                if s.split_group is not None:
                    x_low()
                if s.mask_group is not None:
                    mask(s.mask_group, s.mask_buf)
                if s.hurried:
                    ln_sigma(s.n - 1)
                    if s.final is not None:
                        out_rstd(s.final + 1)
                    ln_gain(s.n - 1, s.prev_layer)
                    ln_offset(s.n - 1, s.prev_layer)
                    for b in range(G):
                        hlin_low(b)
                    return
                if s.final is not None:
                    out_rstd(s.final + 1)
                hlin_low(0)
                if prev:
                    ln_sigma(s.n - 1)
                hlin_low(1)
                hlin_low(2)
                hlin_low(3)
                if prev:
                    ln_gain(s.n - 1, s.prev_layer)
                    ln_offset(s.n - 1, s.prev_layer)

            for constant, value in ((half, 0.5), (minus_half, -0.5), (unbiased, H / (H - 1.0)),
                                    (out_eps, OUT_EPS)):
                nc.gpsimd.memset(constant[:], value).then_inc(scalars_set, 1)
            nc.gpsimd.memset(hlin_hi[:, :, H:].bitcast(F32), 1.0).then_inc(ones_set, 1)
            nc.gpsimd.memset(hlin_lo[:, :, H:].bitcast(F32), 0.0).then_inc(ones_set, 1)
            pool.wait_ge(consts_in, 5 * DMA)
            mask(0, 0)
            pool.wait_ge(scalars_set, 4)
            head = head_slots()
            slot(head[0])
            for kind in range(3):
                pool.wait_ge(w_hi1_done, kind + 1)
                nc.gpsimd.tensor_tensor(w_lo[:, 1, kind], raw_w[1][kind], w_hi[:, 1, kind].bitcast(F32),
                                        ALU.subtract).then_inc(w_lo1_done, 1)
            for s in head[1:]:
                slot(s)
            with pool.Fori(0, LOOPS) as r:
                for s in loop_slots(r):
                    slot(s)
            for s in tail_slots():
                slot(s)
            out_rstd(NG - 1)
            ln_sigma(UNITS - 1)
            out_rstd(NG, 0, 2)
            out_rstd(NG + 1, 2, 4)


def kernel(x, adj, L0_gnn_W_left, L0_gnn_W_right, L0_gnn_W_lin, L0_gnn_b_lin, L0_gnn_ln_a, L0_gnn_ln_b):
    import numpy as np
    import concourse.bacc as bacc
    from concourse.bass_utils import run_bass_kernel_spmd

    x, adj = np.asarray(x), np.asarray(adj)
    x_tok = x.reshape(NG, G, S, H).transpose(0, 2, 1, 3)
    x_feat = x.reshape(NG, G, S, HC, P).transpose(0, 4, 3, 1, 2).reshape(NG, P, HC, TOK)
    adj_tok = adj.reshape(NG, G, S, S).transpose(0, 2, 1, 3)
    adj_t = adj.reshape(NG, G, S, S).transpose(0, 3, 1, 2)
    w_lin_t = np.asarray(L0_gnn_W_lin).transpose(0, 2, 1)
    w = np.stack([np.asarray(L0_gnn_W_left), np.asarray(L0_gnn_W_right), w_lin_t], axis=1)
    w_feat = w.reshape(L, 3, HC, P, H).transpose(0, 1, 3, 2, 4)
    arrays = {
        "x_tok": x_tok, "x_feat": x_feat, "adj_pair": np.stack([adj_t, adj_tok], axis=2),
        "w_feat": w_feat, "b_lin": L0_gnn_b_lin, "ln_a": L0_gnn_ln_a, "ln_b": L0_gnn_ln_b,
        "identity_in": np.eye(S, dtype=np.float32),
        "triangles_in": np.stack([np.tril(np.ones((S, S), np.float32)),
                                  np.triu(np.ones((S, S), np.float32), 1)], axis=1),
    }
    nc = bacc.Bacc("TRN2", target_bir_lowering=False, num_devices=1)
    in_map, args = {}, []
    for name, a in arrays.items():
        a = np.ascontiguousarray(a)
        in_map[name + "_dram"] = a
        args.append(nc.dram_tensor(name + "_dram", a.shape, F32, kind="ExternalInput").ap())
    out = nc.dram_tensor("out_dram", (NG, S, G, H), F32, kind="ExternalOutput").ap()
    build(nc, *args, out)
    r = run_bass_kernel_spmd(nc, [in_map], core_ids=[0])
    got = r.results[0]["out_dram"]
    return np.ascontiguousarray(got.transpose(0, 2, 1, 3).reshape(B, S, H))
```
